# Optimizing a Trainium2 kernel written in Bass

```python
import numpy as np
import jax
import jax.numpy as jnp

def _softmax(x, axis=-1):
    return jax.nn.softmax(x, axis=axis)

def _gelu(x):
    return jax.nn.gelu(x, approximate=True)

def _silu(x):
    return jax.nn.silu(x)

def _sigmoid(x):
    return jax.nn.sigmoid(x)

def _layernorm(x, axis=-1, eps=1e-05):
    m = jnp.mean(x, axis=axis, keepdims=True)
    v = jnp.var(x, axis=axis, keepdims=True)
    return (x - m) / jnp.sqrt(v + eps)

def _scatter_add(tgt, idx, src, axis=0):
    return tgt.at[idx].add(src)

def _segment_sum(src, seg, n):
    return jax.ops.segment_sum(src, seg, n)
kernel_name = 'mk_seq_postln_d1_jaxref_r8_224473'

def setup_inputs(seed: int=0):
    np.random.seed(seed)
    _w = jnp.asarray

    def _L0_attn_setup():
        import jax, jax.numpy as jnp
        import numpy as np
        B, S, D = (2, 256, 128)
        H = 16
        HD = D // H
        FORESIGHT = -1000000000.0
        key = jax.random.key(seed)
        ks = jax.random.split(key, 8)
        s = 0.02
        return {'x': jax.random.normal(ks[0], (B, S, D), dtype=jnp.float32), 'Wq': jax.random.normal(ks[1], (D, H * HD), dtype=jnp.float32) * s, 'bq': jax.random.normal(ks[2], (H * HD,), dtype=jnp.float32) * s, 'Wk': jax.random.normal(ks[3], (D, H * HD), dtype=jnp.float32) * s, 'Wv': jax.random.normal(ks[4], (D, H * HD), dtype=jnp.float32) * s, 'Wo': jax.random.normal(ks[5], (H * HD, D), dtype=jnp.float32) * s, 'bo': jax.random.normal(ks[6], (D,), dtype=jnp.float32) * s}
    _L0_attn_in = _L0_attn_setup()

    def _L0_ffn_setup():
        import jax, jax.numpy as jnp
        import numpy as np
        H, I, E, NS, C = (128, 128, 6, 2, 2)
        TOPK = 2
        TEMP = 1.0
        EPS = 1e-06
        key = jax.random.key(seed)
        ks = jax.random.split(key, 20)
        sd = 0.02
        inp = {'x': jax.random.normal(ks[0], (4, 256, H), jnp.float32), 'router_W': jax.random.normal(ks[1], (C, H, E), jnp.float32) * sd, 'router_b': jax.random.normal(ks[2], (C, E), jnp.float32) * sd, 'gate_bias': jax.random.normal(ks[3], (C, E), jnp.float32) * sd, 'exp_Wup': jax.random.normal(ks[4], (E, H, I), jnp.float32) * sd, 'exp_bup': jnp.zeros((E, I), jnp.float32), 'exp_Wg': jax.random.normal(ks[5], (E, I, I), jnp.float32) * sd, 'exp_bg': jnp.zeros((E, I), jnp.float32), 'exp_Wdown': jax.random.normal(ks[6], (E, I, H), jnp.float32) * sd, 'exp_bdown': jnp.zeros((E, H), jnp.float32), 'share_Wup': jax.random.normal(ks[7], (H, NS * I), jnp.float32) * sd, 'share_bup': jnp.zeros((NS * I,), jnp.float32), 'share_Wg': jax.random.normal(ks[8], (I, I), jnp.float32) * sd, 'share_bg': jnp.zeros((I,), jnp.float32), 'share_Wdown': jax.random.normal(ks[9], (I, H), jnp.float32) * sd, 'share_bdown': jnp.zeros((H,), jnp.float32), 'norm_w': jnp.ones((C, H), jnp.float32)}
        return inp
    _L0_ffn_in = _L0_ffn_setup()
    _d = {'L0_attn_x': _L0_attn_in['x'], 'L0_attn_Wq': _L0_attn_in['Wq'], 'L0_attn_bq': _L0_attn_in['bq'], 'L0_attn_Wk': _L0_attn_in['Wk'], 'L0_attn_Wv': _L0_attn_in['Wv'], 'L0_attn_Wo': _L0_attn_in['Wo'], 'L0_attn_bo': _L0_attn_in['bo'], 'L0_ffn_router_W': _L0_ffn_in['router_W'], 'L0_ffn_router_b': _L0_ffn_in['router_b'], 'L0_ffn_gate_bias': _L0_ffn_in['gate_bias'], 'L0_ffn_exp_Wup': _L0_ffn_in['exp_Wup'], 'L0_ffn_exp_bup': _L0_ffn_in['exp_bup'], 'L0_ffn_exp_Wg': _L0_ffn_in['exp_Wg'], 'L0_ffn_exp_bg': _L0_ffn_in['exp_bg'], 'L0_ffn_exp_Wdown': _L0_ffn_in['exp_Wdown'], 'L0_ffn_exp_bdown': _L0_ffn_in['exp_bdown'], 'L0_ffn_share_Wup': _L0_ffn_in['share_Wup'], 'L0_ffn_share_bup': _L0_ffn_in['share_bup'], 'L0_ffn_share_Wg': _L0_ffn_in['share_Wg'], 'L0_ffn_share_bg': _L0_ffn_in['share_bg'], 'L0_ffn_share_Wdown': _L0_ffn_in['share_Wdown'], 'L0_ffn_share_bdown': _L0_ffn_in['share_bdown'], 'L0_ffn_norm_w': _L0_ffn_in['norm_w']}
    _x0 = _d['L0_attn_x']
    _d['L0_attn_x'] = jax.random.normal(jax.random.fold_in(jax.random.key(seed), 1), (8, 256, 128), dtype=_x0.dtype)
    del _x0
    return _d

def reference(L0_attn_x, L0_attn_Wq, L0_attn_bq, L0_attn_Wk, L0_attn_Wv, L0_attn_Wo, L0_attn_bo, L0_ffn_router_W, L0_ffn_router_b, L0_ffn_gate_bias, L0_ffn_exp_Wup, L0_ffn_exp_bup, L0_ffn_exp_Wg, L0_ffn_exp_bg, L0_ffn_exp_Wdown, L0_ffn_exp_bdown, L0_ffn_share_Wup, L0_ffn_share_bup, L0_ffn_share_Wg, L0_ffn_share_bg, L0_ffn_share_Wdown, L0_ffn_share_bdown, L0_ffn_norm_w):

    def _L0_attn_ref(x, Wq, bq, Wk, Wv, Wo, bo):
        import jax, jax.numpy as jnp
        import numpy as np
        B, S, D = (2, 256, 128)
        H = 16
        HD = D // H
        FORESIGHT = -1000000000.0
        b, s, _ = x.shape
        q = (x @ Wq + bq).reshape(b, s, H, HD).transpose(0, 2, 1, 3)
        k = (x @ Wk).reshape(b, s, H, HD).transpose(0, 2, 1, 3)
        v = (x @ Wv).reshape(b, s, H, HD).transpose(0, 2, 1, 3)
        scores = jnp.einsum('bhqd,bhkd->bhqk', q, k) / jnp.sqrt(jnp.float32(HD))
        slopes = 2.0 ** (-8.0 * jnp.arange(1, H + 1, dtype=jnp.float32) / H)
        positions = jnp.arange(s, dtype=jnp.float32)
        scores = scores - slopes[None, :, None, None] * positions[None, None, None, :]
        causal = jnp.tril(jnp.ones((s, s), dtype=bool))
        scores = jnp.where(causal[None, None, :, :], scores, FORESIGHT)
        attn = jax.nn.softmax(scores, axis=-1)
        out = jnp.einsum('bhqk,bhkd->bhqd', attn, v)
        out = out.transpose(0, 2, 1, 3).reshape(b, s, H * HD)
        return out @ Wo + bo

    def _L0_ffn_ref(x, router_W, router_b, gate_bias, exp_Wup, exp_bup, exp_Wg, exp_bg, exp_Wdown, exp_bdown, share_Wup, share_bup, share_Wg, share_bg, share_Wdown, share_bdown, norm_w):
        import jax, jax.numpy as jnp
        import numpy as np
        H, I, E, NS, C = (128, 128, 6, 2, 2)
        TOPK = 2
        TEMP = 1.0
        EPS = 1e-06
        B, S, Hd = x.shape
        xf = x.reshape(-1, Hd)
        for j in range(C):
            residual = xf
            gate = (xf @ router_W[j] + router_b[j]) / TEMP
            biased = gate + gate_bias[j]
            _, ids = jax.lax.top_k(biased, TOPK)
            sel = (ids[:, :, None] == jnp.arange(E)[None, None, :]).any(axis=1)
            weights = jax.nn.softmax(jnp.where(sel, gate, -jnp.inf), axis=-1)
            h = jnp.einsum('nh,ehi->eni', xf, exp_Wup) + exp_bup[:, None, :]
            h = jax.nn.silu(jnp.einsum('eni,eij->enj', h, exp_Wg) + exp_bg[:, None, :]) * h
            eo = jnp.einsum('eni,eih->enh', h, exp_Wdown) + exp_bdown[:, None, :]
            combined = jnp.einsum('ne,enh->nh', weights, eo)
            s = (xf @ share_Wup + share_bup).reshape(-1, NS, I)
            s = jax.nn.silu(s @ share_Wg + share_bg) * s
            share_out = (s @ share_Wdown + share_bdown).sum(axis=1)
            z = combined + share_out
            y = residual + z
            y = y * jax.lax.rsqrt(jnp.mean(y * y, axis=-1, keepdims=True) + EPS) * norm_w[j]
            xf = y
        return xf.reshape(B, S, Hd)
    x = L0_attn_x
    x = _layernorm(x + _L0_attn_ref(x, L0_attn_Wq, L0_attn_bq, L0_attn_Wk, L0_attn_Wv, L0_attn_Wo, L0_attn_bo), axis=-1)
    x = _layernorm(x + _L0_ffn_ref(x, L0_ffn_router_W, L0_ffn_router_b, L0_ffn_gate_bias, L0_ffn_exp_Wup, L0_ffn_exp_bup, L0_ffn_exp_Wg, L0_ffn_exp_bg, L0_ffn_exp_Wdown, L0_ffn_exp_bdown, L0_ffn_share_Wup, L0_ffn_share_bup, L0_ffn_share_Wg, L0_ffn_share_bg, L0_ffn_share_Wdown, L0_ffn_share_bdown, L0_ffn_norm_w), axis=-1)
    return x

_drawn_inputs = setup_inputs


def setup_inputs(seed=0):
    import zlib

    import numpy as np

    out = dict(_drawn_inputs(seed))
    spreads = {'L0_ffn_exp_bup': (0.0, 0.8),
     'L0_ffn_exp_bg': (0.0, 0.8),
     'L0_ffn_exp_bdown': (0.0, 0.298),
     'L0_ffn_share_bup': (0.0, 0.8),
     'L0_ffn_share_bg': (0.0, 0.8),
     'L0_ffn_share_bdown': (0.0, 0.313),
     'L0_ffn_norm_w': (1.0, 0.2)}
    factors = {'L0_attn_Wq': 8.0,
     'L0_attn_bq': 8.0,
     'L0_attn_Wk': 8.0,
     'L0_attn_Wv': 3.725,
     'L0_attn_Wo': 3.662,
     'L0_ffn_router_b': 5.162,
     'L0_ffn_gate_bias': 4.395,
     'L0_ffn_exp_Wup': 8.0,
     'L0_ffn_exp_Wg': 8.0,
     'L0_ffn_exp_Wdown': 8.0,
     'L0_ffn_share_Wup': 8.0,
     'L0_ffn_share_Wg': 8.0,
     'L0_ffn_share_Wdown': 8.0}
    for name, (base, spread) in spreads.items():
        noise = np.random.default_rng([zlib.crc32(name.encode()), seed]).standard_normal(out[name].shape)
        drawn = base * np.exp(spread * noise) if base else spread * noise
        out[name] = jnp.asarray(drawn.astype(out[name].dtype))
    for name, factor in factors.items():
        out[name] = (out[name] * factor).astype(out[name].dtype)
    return out
```

```python
from contextlib import ExitStack

import concourse.bass as bass
from concourse import mybir

F32 = mybir.dt.float32
F32R = mybir.dt.float32r
BF16 = mybir.dt.bfloat16
ALU = mybir.AluOpType
ACT = mybir.ActivationFunctionType
AX = mybir.AxisListType

P = 128
B, S, D = 8, 256, 128
H, HD = 16, 8
TB = S // P
NT = B * TB
GT = 4
NG = NT // GT
GW = GT * P
U = 4
HU = H // U
NBANK = 3 * U
ROWS_QK = 3 * HD
ROWS_MAX = 96
ROWS_EXP = 128
QSCALE = float(HD) ** -0.5
LN_EPS = 1e-5
C, E, TOPK = 2, 6, 2
NS = 2
N = E + NS
FF_EPS = 1e-6
ROUTER_STEPS = 14
PREP_T, PREP_G, PREP_W = 1, 3, 6


def program(nc, x, Wq, bq, Wk, Wv, Wo, bo, router_W, router_b, gate_bias, exp_Wup, exp_bup, exp_Wg, exp_bg,
            exp_Wdown, exp_bdown, share_Wup, share_bup, share_Wg, share_bg, share_Wdown, share_bdown, norm_w,
            ident_c, causal_c, alibi_c, unit_c, before_c, out):
    ctx = ExitStack()
    with ctx:
        def sb(name, shape, dt=F32):
            return ctx.enter_context(nc.sbuf_tensor(name, shape, dt))

        def sem(name):
            return ctx.enter_context(nc.semaphore(name))

        banks = ctx.enter_context(nc.psum_tensor("banks", [P, 8, 512], F32))

        ident = sb("ident", [P, P])
        ident_bf = sb("ident_bf", [P, P], BF16)
        causal = sb("causal", [P, P])
        step = sb("step", [1, 2])
        causal_bf = sb("causal_bf", [P, 4, P], BF16)
        w_in = sb("w_in", [P, 3, P])
        wqs = sb("wqs", [P, P])
        w_hi = sb("w_hi", [P, 3, P], F32R)
        w_lo = sb("w_lo", [P, 3, P], F32R)
        wo = sb("wo", [P, P])
        bo_all = sb("bo_all", [P, P])
        bq_row = sb("bq_row", [1, P])
        bq_perm = sb("bq_perm", [1, P])
        scale_one = sb("scale_one", [1, 1])
        bq_col = sb("bq_col", [P, 1])
        minus_half = sb("minus_half", [P, GT])

        x_sb = sb("x_sb", [P, NT, D])
        xb_sb = sb("xb_sb", [P, NT, D])
        v_sb = sb("v_sb", [P, NT, D])
        x1 = sb("x1", [P, NT, D])
        xT_hi = sb("xT_hi", [P, 2, GW], F32R)
        xT_lo = sb("xT_lo", [P, 2, GW], F32R)
        q_hi = sb("q_hi", [P, 2, GW], F32R)
        q_lo = sb("q_lo", [P, 2, GW], F32R)
        k_hi = sb("k_hi", [P, 2, GW], F32R)
        k_lo = sb("k_lo", [P, 2, GW], F32R)

        up_w = sb("up_w", [P, N, P])
        gate_w = sb("gate_w", [P, E + 1, P])
        up_t = sb("up_t", [P, N, P])
        down_w = sb("down_w", [P, E + 1, P])
        up_hi = sb("up_hi", [P, N, P], F32R)
        up_lo = sb("up_lo", [P, N, P], F32R)
        gate_hi = sb("gate_hi", [P, N, P], F32R)
        gate_lo = sb("gate_lo", [P, N, P], F32R)
        down_b = sb("down_b", [2 * E + 1, P])
        b_rows = sb("b_rows", [2 * E + NS + 1, P])
        b_cols = sb("b_cols", [P, 2 * E + NS + 1])
        gate_b = sb("gate_b", [P, N])
        unit_rows = sb("unit_rows", [2 * E, E * P])
        unit_rows_r = sb("unit_rows_r", [2 * E, E, P], F32R)
        before = sb("before", [P, E * E])
        rout_w = sb("rout_w", [P, C, E])
        rout_hi = sb("rout_hi", [P, C, E], F32R)
        rout_lo = sb("rout_lo", [P, C, E], F32R)
        rout_b = sb("rout_b", [P, C, E])
        rout_gb = sb("rout_gb", [P, C, E])
        norm_all = sb("norm_all", [P, C, D])

        attention = ExitStack()

        def sba(name, shape, dt=F32):
            return attention.enter_context(nc.sbuf_tensor(name, shape, dt))

        q_st = [sba(f"q_st{p}", [P, H, S], F32R) for p in range(2)]
        k_st = [sba(f"k_st{p}", [P, H, S], F32R) for p in range(2)]
        v_st = [sba(f"v_st{p}", [P, TB, H, 32]) for p in range(2)]
        m_neg = sba("m_neg", [P, TB, H])
        m_split = sba("m_split", [P, TB, 2 * H], F32R)
        m_rows = sba("m_rows", [2 * H, S], F32R)
        probs = [sba(f"probs{r}", [P, HU * S + HU * P]) for r in range(2)]
        o_t = [sba(f"o_t{p}", [P, U, S]) for p in range(2)]
        den_inv = sba("den_inv", [P, H])
        o_norm = sba("o_norm", [P, TB, D])
        o_norm_t = sba("o_norm_t", [P, S])
        res1 = sba("res1", [P, TB, D])
        stats1 = sba("stats1", [P, TB, 6])
        mv1 = sba("mv1", [P, TB, 2])
        var1 = sba("var1", [P, TB])
        rstd1 = sba("rstd1", [P, TB])

        attention.close()
        x_in = [sb(f"x_in{q}", [P, GT, D]) for q in range(2)]
        y_out = [sb(f"y_out{q}", [P, GT, D]) for q in range(2)]
        y_sum = [sb(f"y_sum{q}", [P, GT, D]) for q in range(2)]
        y_end = [sb(f"y_end{q}", [P, GT, D]) for q in range(2)]
        x_end = [sb(f"x_end{q}", [P, GT, D]) for q in range(2)]
        f_hi = [sb(f"f_hi{q}", [P, GW], F32R) for q in range(2)]
        f_lo = [sb(f"f_lo{q}", [P, GW], F32R) for q in range(2)]
        silu = [sb(f"silu{r}", [P, GW]) for r in range(2)]
        hid = [sb(f"hid{r}", [P, GW]) for r in range(2)]
        hid_w = [sb(f"hid_w{r}", [P, GW]) for r in range(2)]
        hid_s = [sb(f"hid_s{r}", [P, GW]) for r in range(2)]
        hid_sum = sb("hid_sum", [P, GW])
        squares = sb("squares", [P, GT, D])
        g_val = sb("g_val", [P, GT, E])
        g_bias = sb("g_bias", [P, GT, E])
        beats = sb("beats", [P, GT, E, E])
        ties = sb("ties", [P, GT, E, E])
        rank = sb("rank", [P, GT, E])
        half_sel = sb("half_sel", [P, GT, E])
        sel_g = sb("sel_g", [P, GT, E])
        half_sum = sb("half_sum", [P, GT])
        g_diff = sb("g_diff", [P, GT, E])
        g_tanh = sb("g_tanh", [P, GT, E])
        w_tok = sb("w_tok", [P, GT, E])
        w_tok_s = sb("w_tok_s", [P, GT, 2 * E], F32R)
        w_t = [sb(f"w_t{q}", [2 * E + 1, GW], F32R) for q in range(2)]
        ssq = sb("ssq", [P, GT])
        ms = sb("ms", [P, GT])
        rms_inv = sb("rms_inv", [P, GT])
        stats2 = sb("stats2", [P, GT, 6])
        mv2 = sb("mv2", [P, GT, 2])
        var2 = sb("var2", [P, GT])
        rstd2 = sb("rstd2", [P, GT])

        q_rows = nc.dram_tensor("q_rows", [3, HD * H, B * S], F32, kind="Internal").ap()
        const_rows = nc.dram_tensor("const_rows", [4 + 2 * H, H, S], F32, kind="Internal").ap()
        k_rows = nc.dram_tensor("k_rows", [3, HD * H, B * S], F32, kind="Internal").ap()

        x_loaded = [sem(f"x_loaded{g}") for g in range(NG)]
        w_loaded = sem("w_loaded")
        c_loaded = sem("c_loaded")
        cast_done = sem("cast_done")
        w_split = sem("w_split")
        bq_cols = sem("bq_cols")
        bq_made = sem("bq_made")
        bq_ready = sem("bq_ready")
        ones_ready = sem("ones_ready")
        xb_ready = sem("xb_ready")
        st_zero = sem("st_zero")
        const_copied = sem("const_copied")
        const_in = sem("const_in")
        xT_done = sem("xT_done")
        xhi_done = sem("xhi_done")
        xlo_done = sem("xlo_done")
        qkv_done = sem("qkv_done")
        qkh_done = sem("qkh_done")
        qkl_done = sem("qkl_done")
        v_copied = sem("v_copied")
        rows_out = [sem(f"rows_out{g}") for g in range(NG)]
        st_in = [[sem(f"st_in{p}{u}") for u in range(U)] for p in range(2)]
        s_done = sem("s_done")
        max_done = sem("max_done")
        m_hi = sem("m_hi")
        m_lo = sem("m_lo")
        mT_done = sem("mT_done")
        mT_copied = sem("mT_copied")
        m_in = [[sem(f"m_in{p}{u}") for u in range(U)] for p in range(2)]
        st_done = sem("st_done")
        exp_done = sem("exp_done")
        sel_done = sem("sel_done")
        step_done = sem("step_done")
        v_ready = sem("v_ready")
        v_const = sem("v_const")
        av_done = sem("av_done")
        ot_copied = sem("ot_copied")
        oT_done = sem("oT_done")
        den_done = sem("den_done")
        norm_done = sem("norm_done")
        onT_done = sem("onT_done")
        onT_copied = sem("onT_copied")
        proj_done = sem("proj_done")
        res1_done = sem("res1_done")
        bn1_done = sem("bn1_done")
        mv1_done = sem("mv1_done")
        var1_done = sem("var1_done")
        rstd1_done = sem("rstd1_done")
        x1_done = sem("x1_done")
        out_done = [sem(f"out_done{q}") for q in range(2)]
        fw_in = sem("fw_in")
        upT_done = sem("upT_done")
        upT_copied = sem("upT_copied")
        wg_made = sem("wg_made")
        fw_hi = sem("fw_hi")
        fw_lo = sem("fw_lo")
        bcol_done = sem("bcol_done")
        bcol_copied = sem("bcol_copied")
        bg_made = sem("bg_made")
        gb_ready = sem("gb_ready")
        rw_split = sem("rw_split")
        wt_ready = sem("wt_ready")
        xin_ready = sem("xin_ready")
        fT_done = sem("fT_done")
        fhi_done = sem("fhi_done")
        flo_done = sem("flo_done")
        gates_done = sem("gates_done")
        rt = sem("rt")
        tanh_done = sem("tanh_done")
        wtok_done = sem("wtok_done")
        wT_done = sem("wT_done")
        wT_copied = sem("wT_copied")
        gate_done = sem("gate_done")
        up_done = sem("up_done")
        wb_done = sem("wb_done")
        silu_done = sem("silu_done")
        hid_done = sem("hid_done")
        hidw_done = sem("hidw_done")
        hsum_done = sem("hsum_done")
        down_done = sem("down_done")
        ysum_done = sem("ysum_done")
        ssq_done = sem("ssq_done")
        ms_done = sem("ms_done")
        rms_done = sem("rms_done")
        y_done = sem("y_done")
        xend_done = sem("xend_done")
        bn2_done = sem("bn2_done")
        mv2_done = sem("mv2_done")
        var2_done = sem("var2_done")
        rstd2_done = sem("rstd2_done")
        o_ready = sem("o_ready")

        def wait(eng, s, value):
            if not isinstance(value, int) or value > 0:
                eng.wait_ge(s, value)

        from_1 = {"pe": (oT_done, onT_done, proj_done, av_done, down_done),
                  "dve": (res1_done, norm_done, x1_done, hid_done, ms_done, bn2_done, var2_done, hidw_done, ysum_done, flo_done),
                  "act": (silu_done, wT_copied),
                  "pool": (rstd1_done, hsum_done, xend_done)}

        def wait_from_1(eng, s, value):
            if not isinstance(value, int) or value > 0:
                eng.wait_ge(s, value + 1)

        def start_from_1(eng, name):
            for s in from_1[name]:
                eng.sem_inc(s, 1)

        max_bank = [banks[:, 0, :], banks[:, 1, :]]
        exp_bank0 = banks[:, 2:4, :].rearrange("p a c -> p (a c)")
        exp_bank1 = banks[:, 4, :]
        av_bank = [banks[:, 5, 0:S], banks[:, 6, 0:S]]
        misc = banks[:, 7, :]

        gate_bank, up_bank, wb_bank, fT_bank = (banks[:, n, :] for n in range(4))
        rout_bank, wT_bank = banks[:, 4, 0:GT * E], banks[0:2 * E, 5, :]
        down_bank = [banks[:, 6, :], banks[:, 7, :]]

        def steps_of(pair):
            return [(4 * pair + n, n % 2, n // 2) for n in range(4)]

        block = ctx.enter_context(nc.Block())

        @block.sync
        def _(sp):
            x_tiles = x.rearrange("b (u p) d -> p (b u) d", p=P)
            for g in range(NG):
                sp.dma_start(x_sb[:, GT * g:GT * g + GT, :], x_tiles[:, GT * g:GT * g + GT, :]).then_inc(x_loaded[g], 16)
            sp.dma_start(bo_all[:], bo.rearrange("(o d) -> o d", o=1).broadcast_to((P, D))).then_inc(c_loaded, 16)
            sp.dma_start(wo[:], Wo).then_inc(c_loaded, 16)
            sp.dma_start(up_w[:, 0:E, :], exp_Wup.rearrange("e h i -> h e i")).then_inc(fw_in, 16)
            sp.dma_start(up_w[:, E:N, :], share_Wup.rearrange("h (s i) -> h s i", s=NS)).then_inc(fw_in, 16)
            sp.dma_start(gate_w[:, 0:E, :], exp_Wg.rearrange("e h i -> h e i")).then_inc(fw_in, 16)
            sp.dma_start(gate_w[:, E, :], share_Wg).then_inc(fw_in, 16)
            sp.dma_start(down_w[:, 0:E, :], exp_Wdown.rearrange("e h i -> h e i")).then_inc(fw_in, 16)
            sp.dma_start(down_w[:, E, :], share_Wdown).then_inc(fw_in, 16)
            for n in range(2):
                sp.dma_start(down_b[E * n:E * n + E, :], exp_bdown).then_inc(fw_in, 16)
            sp.dma_start(down_b[2 * E:2 * E + 1, :], share_bdown.rearrange("(o d) -> o d", o=1)).then_inc(fw_in, 16)
            sp.dma_start(b_rows[0:E, :], exp_bup).then_inc(fw_in, 16)
            sp.dma_start(b_rows[E:2 * E, :], exp_bg).then_inc(fw_in, 16)
            sp.dma_start(b_rows[2 * E:2 * E + NS, :], share_bup.rearrange("(s d) -> s d", s=NS)).then_inc(fw_in, 16)
            sp.dma_start(b_rows[2 * E + NS:2 * E + NS + 1, :], share_bg.rearrange("(o d) -> o d", o=1)).then_inc(fw_in, 16)
            sp.dma_start(unit_rows[:], unit_c).then_inc(fw_in, 16)
            sp.dma_start(before[:], before_c).then_inc(fw_in, 16)
            sp.dma_start(rout_w[:], router_W.rearrange("c h e -> h c e")).then_inc(fw_in, 16)
            for dst, src in ((rout_b, router_b), (rout_gb, gate_bias), (norm_all, norm_w)):
                sp.dma_start(dst[:], src.rearrange("(o c) e -> o c e", o=1).broadcast_to((P, C, src.shape[1]))).then_inc(fw_in, 16)

            def rows_to_dram(g):
                sp.wait_ge(qkh_done, 2 * g + 2)
                sp.wait_ge(qkl_done, 2 * g + 2)
                for dst, parts in ((q_rows, (q_hi, q_hi, q_lo)), (k_rows, (k_hi, k_lo, k_hi))):
                    for n, part in enumerate(parts):
                        sp.dma_start(dst[n, :, g * GW:(g + 1) * GW], part[:, g % 2, :].bitcast(F32)).then_inc(rows_out[g], 16)

            def stacks_in(b, p, u):
                for dst, src in ((q_st, q_rows), (k_st, k_rows)):
                    sp.dma_start(dst[p][0:24, HU * u:HU * (u + 1), :].bitcast(F32),
                                 src[:, :, bass.ds(b * S, S)].rearrange("n (d h) t -> (n d) h t", h=H)[:, HU * u:HU * (u + 1), :]
                                 ).then_inc(st_in[p][u], 16)

            rows_to_dram(0)
            sp.wait_ge(rows_out[0], 96)
            sp.wait_ge(st_zero, 4)
            for b in range(2):
                for u in range(U):
                    stacks_in(b, b, u)
            for g in range(1, NG):
                rows_to_dram(g)
            for g in range(1, NG):
                sp.wait_ge(rows_out[g], 96)
            with sp.Fori(1, B // 2) as pair:
                for p in range(2):
                    for u in range(U):
                        sp.wait_ge(st_done, 8 * (2 * pair + p - 2) + 2 * u + 2)
                        stacks_in(2 * pair + p, p, u)
            out_tiles = out.rearrange("b (u p) d -> p (b u) d", p=P)
            with sp.Fori(0, NG // 2) as pair:
                for q in range(2):
                    sp.wait_ge(o_ready, 2 * pair + q + 1)
                    sp.dma_start(out_tiles[:, bass.ds((2 * pair + q) * GT, GT), :], xb_sb[:, bass.ds((2 * pair + q) * GT, GT), :]).then_inc(out_done[q], 16)
            for q in range(2):
                sp.wait_ge(out_done[q], 16 * (NG // 2))

        @block.gpsimd
        def _(pool):
            start_from_1(pool, "pool")
            for st in (q_st[0], k_st[0]):
                pool.memset(st[:].bitcast(F32), 0.0).then_inc(st_zero, 1)
            for p in range(2):
                pool.memset(v_st[p][:], 0.0).then_inc(v_const, 1)
            pool.wait_ge(v_const, 2)
            for p in range(2):
                pool.memset(v_st[p][:, :, :, HD:HD + 1], 1.0).then_inc(v_const, 1)
            pool.memset(minus_half[:], -0.5).then_inc(ones_ready, 1)
            pool.memset(step[:], 1.0).then_inc(ones_ready, 1)
            pool.wait_ge(ones_ready, 2)
            pool.memset(scale_one[:], QSCALE).then_inc(ones_ready, 1)
            pool.wait_ge(v_const, 4)
            pool.wait_ge(c_loaded, 16 * 5)
            for g in range(NG):
                pool.wait_ge(x_loaded[g], 16)
                pool.tensor_tensor(xb_sb[:, GT * g:GT * g + GT, :], x_sb[:, GT * g:GT * g + GT, :],
                                   bo_all[:].rearrange("p (o d) -> p o d", o=1).broadcast_to((P, GT, D)), ALU.add).then_inc(xb_ready, 1)

            def stage_v(b, p):
                wait_from_1(pool, av_done, 4 * (b - 1))
                pool.tensor_copy(v_st[p][:, :, :, 0:HD], v_sb[:, bass.ds(b * TB, TB), :].rearrange("p t (h d) -> p t h d", h=H)).then_inc(v_ready, 1)

            def causal_select(n, r, half):
                pool.wait_ge(exp_done, 2 * n + half + 1)
                wait(pool, step_done, 2 * n + half)
                pool.tensor_tensor(step[:, 1:2], step[:, 0:1], step[:, 0:1], ALU.mult).then_inc(step_done, 1)
                v = probs[r][:, half * HU * S:half * HU * S + HU * (P if half else S)].rearrange("p (h q) -> p h q", h=HU)[:, :, 0:P]
                pool.affine_select(out=v, in_=v, compare_op=ALU.is_ge, fill=0.0, base=0,
                                   pattern=[[0, HU], [1, P]], channel_multiplier=-1).then_inc(sel_done, 1)

            def rstd(b):
                pool.wait_ge(var1_done, b + 1)
                pool.tensor_tensor(rstd1[:], var1[:], minus_half[:, 0:TB], ALU.pow).then_inc(rstd1_done, 1)

            def batch(b, p, first, last):
                for u in range(U):
                    for half in range(2):
                        causal_select(4 * b + u, u % 2, half)
                    if u == 1 and not last:
                        stage_v(b + 1, 1 - p)
                if not first:
                    rstd(b - 1)

            pool.wait_ge(v_copied, 1)
            stage_v(0, 0)
            pool.wait_ge(v_copied, NG)
            batch(0, 0, True, False)
            with pool.Fori(0, B // 2 - 1) as pair:
                batch(2 * pair + 1, 1, False, False)
                batch(2 * pair + 2, 0, False, False)
            batch(B - 1, 1, False, True)
            rstd(B - 1)

            def stage_x(group, q):
                pool.tensor_copy(x_in[q][:], x1[:, bass.ds(group * GT, GT), :]).then_inc(xin_ready, 1)

            def power(dst, src, produced, count, done):
                wait_from_1(pool, produced, count)
                pool.tensor_tensor(dst[:], src[:], minus_half[:], ALU.pow).then_inc(done, 1)

            wait_from_1(pool, x1_done, B)
            wait_from_1(pool, av_done, 4 * B)
            wait_from_1(pool, oT_done, 2 * B)
            wait_from_1(pool, proj_done, B)
            for q in range(2):
                pool.memset(w_t[q][:].bitcast(F32), 2.0).then_inc(wt_ready, 1)
            stage_x(0, 0)
            with pool.Fori(0, NG // 2) as pair:
                for s, q, rnd in steps_of(pair):
                    if rnd == 0 and q == 0:
                        wait_from_1(pool, xend_done, 2 * pair)
                        stage_x(2 * pair + 1, 1)
                    wait_from_1(pool, hid_done, N * (s + 1))
                    wait_from_1(pool, down_done, (E + 1) * s)
                    pool.tensor_tensor(hid_sum[:], hid_s[0][:], hid_s[1][:], ALU.add).then_inc(hsum_done, 1)
                    power(rms_inv, ms, ms_done, s + 1, rms_done)
                    if rnd == C - 1:
                        pool.wait_ge(y_done, s + 1)
                        pool.tensor_tensor(x_end[q][:], x_in[q][:], y_end[q][:], ALU.add).then_inc(xend_done, 1)
                        if q == 0:
                            wait_from_1(pool, xend_done, 2 * pair + 1)
                            stage_x((2 * pair + 2) % NG, 0)
                        power(rstd2, var2, var2_done, 2 * pair + q + 1, rstd2_done)

        @block.scalar
        def _(act):
            start_from_1(act, "act")
            for n, w in enumerate((Wq, Wk, Wv)):
                act.dma_start(w_in[:, n, :], w).then_inc(w_loaded, 16)
            act.dma_start(ident[:], ident_c).then_inc(c_loaded, 16)
            act.dma_start(causal[:], causal_c).then_inc(c_loaded, 16)
            act.dma_start(bq_row[:], bq.rearrange("(o d) -> o d", o=1)).then_inc(c_loaded, 16)
            act.dma_start(const_rows, alibi_c).then_inc(const_copied, 16)
            act.wait_ge(bq_made, 1)
            act.copy(bq_col[:], banks[:, 7, 0:1]).then_inc(bq_ready, 1)
            act.wait_ge(bq_ready, 1)
            for g in range(NG):
                act.wait_ge(xT_done, g + 1)
                wait(act, qkv_done, 3 * (g - 1))
                act.copy(xT_hi[:, g % 2, :], banks[:, g % 2, :]).then_inc(xhi_done, 1)
                if g >= 2:
                    act.wait_ge(rows_out[g - 2], 96)
                act.wait_ge(qkv_done, 3 * g + 1)
                act.activation(q_hi[:, g % 2, :], banks[:, 2, :], ACT.Identity, bias=bq_col[:]).then_inc(qkh_done, 1)
                act.wait_ge(qkv_done, 3 * g + 2)
                act.copy(k_hi[:, g % 2, :], banks[:, 3, :]).then_inc(qkh_done, 1)
                act.wait_ge(qkv_done, 3 * g + 3)
                act.copy(v_sb[:, GT * g:GT * g + GT, :].rearrange("p t d -> p (t d)"), banks[:, 4, :]).then_inc(v_copied, 1)
                if g == 0:
                    act.wait_ge(const_copied, 16)
                    act.wait_ge(st_zero, 4)
                    for p in range(2):
                        act.dma_start(k_st[p][24:26, :, :].bitcast(F32), const_rows[0:2]).then_inc(const_in, 16)
                        act.dma_start(q_st[p][24:26, :, :].bitcast(F32), const_rows[2:4]).then_inc(const_in, 16)
                        act.dma_start(k_st[p][ROWS_MAX:ROWS_EXP, :, :].bitcast(F32), const_rows[4:4 + 2 * H]).then_inc(const_in, 16)

            for half in range(2):
                act.wait_ge(upT_done, half + 1)
                act.copy(up_t[:, 4 * half:4 * half + 4, :].rearrange("p n i -> p (n i)"), banks[:, 5 + half, :]).then_inc(upT_copied, 1)
            act.wait_ge(bcol_done, 1)
            act.copy(b_cols[:], banks[:, 7, 0:2 * E + NS + 1]).then_inc(bcol_copied, 1)
            act.wait_ge(fw_in, 16 * 19)
            act.copy(up_hi[:], up_w[:]).then_inc(fw_hi, 1)
            for half in range(2):
                act.wait_ge(wg_made, half + 1)
                act.copy(gate_hi[:, 4 * half:4 * half + 4, :].rearrange("p n i -> p (n i)"), banks[:, 5 + half, :]).then_inc(fw_hi, 1)

            def exps(n, r):
                for half, bank, lo, w in ((0, exp_bank0, 0, HU * S), (1, exp_bank1, HU * S, HU * P)):
                    act.wait_ge(st_done, 2 * n + half + 1)
                    if not half:
                        wait_from_1(act, av_done, n - 1)
                    act.activation(probs[r][:, lo:lo + w], bank, ACT.Exp).then_inc(exp_done, 1)

            def copy_av(b, p, u):
                n = 4 * b + u
                wait_from_1(act, av_done, n + 1)
                if u == 0:
                    wait_from_1(act, oT_done, 2 * (b - 1))
                act.copy(o_t[p][:, u, :], av_bank[u % 2]).then_inc(ot_copied, 1)

            def m_rows_in(b, p, before):
                act.wait_ge(mT_done, b + 1)
                for u in range(U):
                    wait(act, m_in[1 - p][u], 16 * before)
                act.copy(m_rows[:], misc[0:2 * H, 0:S]).then_inc(mT_copied, 1)
                act.wait_ge(mT_copied, b + 1)
                wait(act, st_done, 8 * (b - 1))
                for u in range(U):
                    act.dma_start(q_st[p][ROWS_MAX:ROWS_EXP, HU * u:HU * (u + 1), :].bitcast(F32),
                                  m_rows[:].bitcast(F32).rearrange("r (o t) -> r o t", o=1).broadcast_to((2 * H, HU, S))).then_inc(m_in[p][u], 16)

            def batch(b, p, nth, first, last):
                if not first:
                    copy_av(b - 1, 1 - p, 3)
                exps(4 * b, 0)
                exps(4 * b + 1, 1)
                copy_av(b, p, 0)
                exps(4 * b + 2, 0)
                if not first:
                    copy_onT(b - 1)
                copy_av(b, p, 1)
                exps(4 * b + 3, 1)
                copy_av(b, p, 2)
                if not last:
                    m_rows_in(b + 1, 1 - p, nth)

            def copy_onT(b):
                wait_from_1(act, onT_done, b + 1)
                wait_from_1(act, proj_done, b)
                act.copy(o_norm_t[:], misc[:, 0:S]).then_inc(onT_copied, 1)

            m_rows_in(0, 0, 0)
            batch(0, 0, 1, True, False)
            with act.Fori(0, B // 2 - 1) as pair:
                batch(2 * pair + 1, 1, pair + 1, False, False)
                batch(2 * pair + 2, 0, pair + 2, False, False)
            batch(B - 1, 1, B // 2, False, True)
            copy_av(B - 1, 1, 3)
            copy_onT(B - 1)

            def high_part(s, q):
                act.wait_ge(fT_done, s + 1)
                act.copy(f_hi[q][:], fT_bank).then_inc(fhi_done, 1)

            def router_tanh(s):
                act.wait_ge(rt, ROUTER_STEPS * s + ROUTER_STEPS - 3)
                act.activation(g_tanh[:], g_diff[:], ACT.Tanh).then_inc(tanh_done, 1)

            def weights_t(s, q):
                act.wait_ge(wT_done, s + 1)
                act.copy(w_t[q][0:2 * E, :], wT_bank).then_inc(wT_copied, 1)

            def squares_of(s, q):
                wait_from_1(act, ysum_done, s + 1)
                wait_from_1(act, ms_done, s)
                for t in range(GT):
                    last = act.activation(squares[:, t, :], y_sum[q][:, t, :], ACT.Square, accum_out=ssq[:, t:t + 1])
                last.then_inc(ssq_done, 1)

            act.wait_ge(xin_ready, 1)
            high_part(0, 0)
            router_tanh(0)
            act.wait_ge(wt_ready, 2)
            weights_t(0, 0)
            with act.Fori(0, NG // 2) as pair:
                for s, q, rnd in steps_of(pair):
                    for e in range(N):
                        act.wait_ge(gate_done, N * s + e + 1)
                        wait_from_1(act, hid_done, N * s + max(e - 1, 0))
                        act.activation(silu[e % 2][:], gate_bank, ACT.Silu, bias=gate_b[:, e:e + 1]).then_inc(silu_done, 1)
                        if e == PREP_T:
                            high_part(s + 1, 1 - q)
                        if e == PREP_G:
                            router_tanh(s + 1)
                        if e == PREP_W:
                            weights_t(s + 1, 1 - q)
                    squares_of(s, q)

        @block.vector
        def _(dve):
            start_from_1(dve, "dve")
            for st in (q_st[1], k_st[1]):
                dve.memset(st[:].bitcast(F32), 0.0).then_inc(st_zero, 1)
            dve.wait_ge(c_loaded, 16 * 5)
            dve.tensor_copy(bq_perm[:].rearrange("o (d h) -> o d h", h=H), bq_row[:].rearrange("o (h d) -> o d h", h=H)).then_inc(bq_cols, 1)
            dve.tensor_copy(ident_bf[:], ident[:]).then_inc(cast_done, 1)
            dve.tensor_copy(causal_bf[:], causal[:].rearrange("p (o d) -> p o d", o=1).broadcast_to((P, 4, P))).then_inc(cast_done, 1)
            dve.wait_ge(w_loaded, 48)
            dve.tensor_scalar(wqs[:], w_in[:, 0, :], QSCALE, None, ALU.mult).then_inc(cast_done, 1)
            dve.wait_ge(cast_done, 3)
            def cols(w, n):
                return w if n == 2 else w.rearrange("p (h d) -> p d h", h=H)

            def as_cols(w, n):
                return w if n == 2 else w.rearrange("p (d h) -> p d h", h=H)
            for n in range(3):
                src = wqs[:] if n == 0 else w_in[:, n, :]
                dve.tensor_copy(as_cols(w_hi[:, n, :], n), cols(src, n)).then_inc(w_split, 1)
                dve.wait_ge(w_split, 2 * n + 1)
                dve.tensor_tensor(as_cols(w_lo[:, n, :], n), cols(src, n), as_cols(w_hi[:, n, :].bitcast(F32), n), ALU.subtract).then_inc(w_split, 1)
            dve.wait_ge(bq_ready, 1)
            for g in range(NG):
                dve.wait_ge(xhi_done, g + 1)
                dve.tensor_tensor(xT_lo[:, g % 2, :], banks[:, g % 2, :], xT_hi[:, g % 2, :].bitcast(F32), ALU.subtract).then_inc(xlo_done, 1)
                dve.wait_ge(qkh_done, 2 * g + 1)
                if g >= 2:
                    dve.wait_ge(rows_out[g - 2], 96)
                dve.scalar_tensor_tensor(out=q_lo[:, g % 2, :], in0=banks[:, 2, :], scalar=bq_col[:], in1=q_hi[:, g % 2, :].bitcast(F32),
                                         op0=ALU.add, op1=ALU.subtract).then_inc(qkl_done, 1)
                dve.wait_ge(qkh_done, 2 * g + 2)
                dve.tensor_tensor(k_lo[:, g % 2, :], banks[:, 3, :], k_hi[:, g % 2, :].bitcast(F32), ALU.subtract).then_inc(qkl_done, 1)

            dve.wait_ge(fw_in, 16 * 19)
            dve.tensor_copy(unit_rows_r[:], unit_rows[:].rearrange("p (e i) -> p e i", e=E)).then_inc(rw_split, 1)
            dve.tensor_copy(rout_hi[:], rout_w[:]).then_inc(rw_split, 1)
            dve.wait_ge(rw_split, 2)
            dve.tensor_tensor(rout_lo[:], rout_w[:], rout_hi[:].bitcast(F32), ALU.subtract).then_inc(rw_split, 1)
            dve.wait_ge(fw_hi, 1)
            dve.tensor_tensor(up_lo[:], up_w[:], up_hi[:].bitcast(F32), ALU.subtract).then_inc(fw_lo, 1)
            for half in range(2):
                dve.wait_ge(fw_hi, 2 + half)
                dve.tensor_tensor(gate_lo[:, 4 * half:4 * half + 4, :].rearrange("p n i -> p (n i)"), banks[:, 5 + half, :],
                                  gate_hi[:, 4 * half:4 * half + 4, :].rearrange("p n i -> p (n i)").bitcast(F32), ALU.subtract).then_inc(fw_lo, 1)
            dve.wait_ge(bg_made, 1)
            dve.tensor_tensor(gate_b[:, 0:E], banks[:, 7, 0:E], b_cols[:, E:2 * E], ALU.add).then_inc(gb_ready, 1)
            dve.tensor_scalar(gate_b[:, E:N], banks[:, 7, E:N], b_cols[:, 2 * E + NS:2 * E + NS + 1], None, ALU.add).then_inc(gb_ready, 1)

            def maxima(b, k):
                u, part = divmod(k, 3)
                dve.wait_ge(s_done, NBANK * b + k + 1)
                if k == 0:
                    wait(dve, m_lo, b)
                if part == 0:
                    dst, heads = m_neg[:, 0, HU * u:HU * u + HU], HU
                else:
                    h0 = HU * u + 2 * (part - 1)
                    dst, heads = m_neg[:, 1, h0:h0 + 2], 2
                dve.tensor_reduce(dst, max_bank[k % 2].rearrange("p (h k) -> p h k", h=heads), AX.X, ALU.max, negate=True).then_inc(max_done, 1)

            def split_m(b):
                dve.wait_ge(max_done, NBANK * (b + 1))
                wait(dve, mT_done, b)
                dve.tensor_copy(m_split[:, :, 0:H], m_neg[:]).then_inc(m_hi, 1)
                dve.wait_ge(m_hi, b + 1)
                dve.tensor_tensor(m_split[:, :, H:2 * H], m_neg[:], m_split[:, :, 0:H].bitcast(F32), ALU.subtract).then_inc(m_lo, 1)

            def normalise(b, t):
                wait_from_1(dve, oT_done, 2 * b + t + 1)
                o = misc.rearrange("p (h c) -> p h c", h=H)
                wait_from_1(dve, norm_done, 2 * b + t)
                dve.reciprocal(den_inv[:], o[:, :, HD]).then_inc(den_done, 1)
                dve.wait_ge(den_done, 2 * b + t + 1)
                if t == 0:
                    wait_from_1(dve, onT_done, b)
                dve.tensor_tensor(o_norm[:, t, :].rearrange("p (h d) -> p h d", h=H), o[:, :, 0:HD],
                                  den_inv[:].rearrange("p (h o) -> p h o", o=1).broadcast_to((P, H, HD)), ALU.mult).then_inc(norm_done, 1)

            def residual(b):
                wait_from_1(dve, proj_done, b + 1)
                wait_from_1(dve, x1_done, b)
                dve.tensor_tensor(res1[:], misc[:, 0:S].rearrange("p (t d) -> p t d", t=TB), xb_sb[:, bass.ds(b * TB, TB), :], ALU.add).then_inc(res1_done, 1)

            def moments(b):
                wait_from_1(dve, res1_done, b + 1)
                for t in range(TB):
                    last = dve.bn_stats(stats1[:, t, :], res1[:, t, :])
                last.then_inc(bn1_done, 1)
                dve.wait_ge(cast_done, 3)
                dve.wait_ge(bn1_done, b + 1)
                for t in range(TB):
                    last = dve.bn_aggr(mv1[:, t, :], stats1[:, t, :])
                last.then_inc(mv1_done, 1)
                dve.wait_ge(mv1_done, b + 1)
                wait_from_1(dve, rstd1_done, b)
                dve.tensor_scalar(var1[:], mv1[:, :, 1], LN_EPS, None, ALU.add).then_inc(var1_done, 1)

            def layernorm(b):
                wait_from_1(dve, rstd1_done, b + 1)
                for t in range(TB):
                    last = dve.tensor_scalar(x1[:, bass.ds(b * TB + t, 1), :].rearrange("p o d -> p (o d)"), res1[:, t, :], mv1[:, t, 0:1], rstd1[:, t:t + 1], ALU.subtract, ALU.mult)
                last.then_inc(x1_done, 1)

            def batch(b, first, last):
                for k in range(NBANK):
                    if not last:
                        maxima(b + 1, k)
                    if k in (3, 6) and not first:
                        normalise(b - 1, k // 4)
                if not first:
                    residual(b - 1)
                if not last:
                    split_m(b + 1)
                if not first:
                    moments(b - 1)
                    layernorm(b - 1)

            dve.wait_ge(xb_ready, NG)
            for k in range(NBANK):
                maxima(0, k)
            split_m(0)
            batch(0, True, False)
            with dve.Fori(1, B - 1) as b:
                batch(b, False, False)
            batch(B - 1, False, True)
            normalise(B - 1, 0)
            normalise(B - 1, 1)
            residual(B - 1)
            moments(B - 1)
            layernorm(B - 1)

            def low_part(s, q):
                dve.wait_ge(fhi_done, s + 1)
                dve.tensor_tensor(f_lo[q][:], fT_bank, f_hi[q][:].bitcast(F32), ALU.subtract).then_inc(flo_done, 1)

            def over_tiles(row):
                return row.rearrange("p (o e) -> p o e", o=1).broadcast_to((P, GT, E))

            def route(s, rnd):
                n = [0]

                def done(ins):
                    n[0] += 1
                    ins.then_inc(rt, 1)

                def ready():
                    dve.wait_ge(rt, ROUTER_STEPS * s + n[0])

                dve.wait_ge(gates_done, s + 1)
                done(dve.tensor_tensor(g_val[:], rout_bank.rearrange("p (t e) -> p t e", t=GT), over_tiles(rout_b[:, rnd, :]), ALU.add))
                ready()
                done(dve.tensor_tensor(g_bias[:], g_val[:], over_tiles(rout_gb[:, rnd, :]), ALU.add))
                ready()
                other = g_bias[:].rearrange("p t (o e) -> p t o e", o=1).broadcast_to((P, GT, E, E))
                own = g_bias[:].rearrange("p t (e o) -> p t e o", o=1).broadcast_to((P, GT, E, E))
                done(dve.tensor_tensor(beats[:], other, own, ALU.is_gt))
                done(dve.tensor_tensor(ties[:], other, own, ALU.is_equal))
                ready()
                flat = ties[:].rearrange("p t e f -> p t (e f)")
                done(dve.tensor_tensor(flat, flat, before[:].rearrange("p (o n) -> p o n", o=1).broadcast_to((P, GT, E * E)), ALU.mult))
                ready()
                done(dve.tensor_tensor(beats[:], beats[:], ties[:], ALU.add))
                ready()
                done(dve.tensor_reduce(rank[:], beats[:], AX.X, ALU.add))
                ready()
                done(dve.tensor_scalar(half_sel[:], rank[:], float(TOPK), 0.5, ALU.is_lt, ALU.mult))
                ready()
                done(dve.tensor_tensor(sel_g[:], half_sel[:], g_val[:], ALU.mult))
                ready()
                done(dve.tensor_reduce(half_sum[:], sel_g[:], AX.X, ALU.add))
                ready()
                done(dve.tensor_tensor(g_diff[:], g_val[:], half_sum[:].rearrange("p (t o) -> p t o", o=1).broadcast_to((P, GT, E)), ALU.subtract))
                assert n[0] == ROUTER_STEPS - 3

            def weigh(s):
                dve.wait_ge(tanh_done, s + 1)
                dve.scalar_tensor_tensor(out=w_tok[:], in0=g_tanh[:], scalar=1.0, in1=half_sel[:], op0=ALU.add, op1=ALU.mult).then_inc(rt, 1)
                dve.wait_ge(rt, ROUTER_STEPS * s + ROUTER_STEPS - 2)
                dve.tensor_copy(w_tok_s[:, :, 0:E], w_tok[:]).then_inc(rt, 1)
                dve.wait_ge(rt, ROUTER_STEPS * s + ROUTER_STEPS - 1)
                dve.tensor_tensor(w_tok_s[:, :, E:2 * E], w_tok[:], w_tok_s[:, :, 0:E].bitcast(F32), ALU.subtract).then_inc(rt, 1)

            def unit(s, e):
                up_b = b_cols[:, e:e + 1] if e < E else b_cols[:, E + e:E + e + 1]
                wait_from_1(dve, silu_done, N * s + e + 1)
                dve.wait_ge(up_done, N * s + e + 1)
                if e >= E:
                    wait_from_1(dve, hsum_done, s)
                    dve.scalar_tensor_tensor(out=hid_s[e - E][:], in0=up_bank, scalar=up_b, in1=silu[e % 2][:], op0=ALU.add, op1=ALU.mult).then_inc(hid_done, 1)
                    return
                dve.scalar_tensor_tensor(out=hid[e % 2][:], in0=up_bank, scalar=up_b, in1=silu[e % 2][:], op0=ALU.add, op1=ALU.mult).then_inc(hid_done, 1)
                wait_from_1(dve, hid_done, N * s + e + 1)
                dve.wait_ge(wb_done, E * s + e + 1)
                wait_from_1(dve, down_done, (E + 1) * s + max(e - 1, 0))
                dve.tensor_tensor(hid_w[e % 2][:], hid[e % 2][:], wb_bank, ALU.mult).then_inc(hidw_done, 1)

            def add_residual(s, q, rnd):
                wait_from_1(dve, down_done, (E + 1) * (s + 1))
                src = x_in[q] if rnd == 0 else y_out[q]
                dve.tensor_tensor(y_sum[q][:].rearrange("p t d -> p (t d)"), down_bank[q], src[:].rearrange("p t d -> p (t d)"), ALU.add).then_inc(ysum_done, 1)

            def mean_square(s):
                dve.wait_ge(ssq_done, s + 1)
                dve.tensor_scalar(ms[:], ssq[:], 1.0 / D, FF_EPS, ALU.mult, ALU.add).then_inc(ms_done, 1)

            def rms_norm(s, q, rnd):
                dve.wait_ge(rms_done, s + 1)
                dst = y_out[q] if rnd == 0 else y_end[q]
                for t in range(GT):
                    last = dve.scalar_tensor_tensor(out=dst[:, t, :], in0=y_sum[q][:, t, :], scalar=rms_inv[:, t:t + 1], in1=norm_all[:, rnd, :], op0=ALU.mult, op1=ALU.mult)
                last.then_inc(y_done, 1)

            def end_moments(g, q):
                wait_from_1(dve, xend_done, g + 1)
                for t in range(GT):
                    last = dve.bn_stats(stats2[:, t, :], x_end[q][:, t, :])
                last.then_inc(bn2_done, 1)
                dve.wait_ge(cast_done, 3)
                wait_from_1(dve, bn2_done, g + 1)
                for t in range(GT):
                    last = dve.bn_aggr(mv2[:, t, :], stats2[:, t, :])
                last.then_inc(mv2_done, 1)
                dve.wait_ge(mv2_done, g + 1)
                dve.tensor_scalar(var2[:], mv2[:, :, 1], LN_EPS, None, ALU.add).then_inc(var2_done, 1)

            def end_norm(g, q):
                dve.wait_ge(rstd2_done, g + 1)
                for t in range(GT):
                    last = dve.tensor_scalar(xb_sb[:, bass.ds(g * GT + t, 1), :].rearrange("p o d -> p (o d)"), x_end[q][:, t, :], mv2[:, t, 0:1], rstd2[:, t:t + 1], ALU.subtract, ALU.mult)
                last.then_inc(o_ready, 1)

            low_part(0, 0)
            route(0, 0)
            weigh(0)
            with dve.Fori(0, NG // 2) as pair:
                for s, q, rnd in steps_of(pair):
                    next_rnd = rnd if q == 0 else 1 - rnd
                    for e in range(N):
                        unit(s, e)
                        if e == PREP_T:
                            low_part(s + 1, 1 - q)
                        if e == PREP_G:
                            route(s + 1, next_rnd)
                        if e == PREP_W:
                            weigh(s + 1)
                    add_residual(s, q, rnd)
                    mean_square(s)
                    rms_norm(s, q, rnd)
                    if rnd == C - 1:
                        end_moments(2 * pair + q, q)
                        end_norm(2 * pair + q, q)

        @block.tensor
        def _(pe):
            start_from_1(pe, "pe")
            pe.wait_ge(c_loaded, 16 * 5)
            pe.wait_ge(ones_ready, 3)
            pe.wait_ge(bq_cols, 1)
            pe.matmul(banks[:, 7, 0:1], bq_perm[:], scale_one[:]).then_inc(bq_made, 1)
            pe.wait_ge(bq_ready, 1)
            pe.wait_ge(w_split, 6)
            PASSES = ((w_hi, xT_hi), (w_hi, xT_lo), (w_lo, xT_hi))

            def transpose_x(g):
                pe.wait_ge(x_loaded[g], 16)
                wait(pe, xlo_done, g - 1)
                for t in range(GT):
                    last = pe.transpose(banks[:, g % 2, P * t:P * t + P], x_sb[:, GT * g + t, :], ident[:])
                last.then_inc(xT_done, 1)

            transpose_x(0)
            for g in range(NG):
                if g + 1 < NG:
                    transpose_x(g + 1)
                pe.wait_ge(xhi_done, g + 1)
                pe.wait_ge(xlo_done, g + 1)
                for n in range(2):
                    wait(pe, qkl_done, 2 * (g - 1) + n + 1)
                    for k, (w, xt) in enumerate(PASSES):
                        last = pe.matmul(banks[:, 2 + n, :], w[:, n, :], xt[:, g % 2, :], start=(k == 0), stop=(k == 2))
                    last.then_inc(qkv_done, 1)
                wait(pe, v_copied, g)
                for t in range(GT):
                    for k, (w, xt) in enumerate(PASSES):
                        last = pe.matmul(banks[:, 4, P * t:P * t + P], xt[:, g % 2, P * t:P * t + P], w[:, 2, :], start=(k == 0), stop=(k == 2))
                last.then_inc(qkv_done, 1)

            def scores_for_max(b, p, nth, k):
                u, part = divmod(k, 3)
                if part == 0:
                    pe.wait_ge(st_in[p][u], 32 * nth)
                wait(pe, max_done, NBANK * b + k - 1)
                bank = max_bank[k % 2]
                if part == 0:
                    heads, width, keys, q0 = HU, P, P, 0
                else:
                    heads, width, keys, q0 = 2, S, S, P
                pe.matmul(bank.rearrange("p (h k) -> p h k", h=heads)[:, :, width - P:width], ident_bf[:], causal_bf[:, 0:heads, :],
                          start=True, stop=False, skip_group_check=True)
                for j in range(heads):
                    h = HU * u + 2 * max(part - 1, 0) + j
                    last = pe.matmul(bank[:, width * j:width * (j + 1)], q_st[p][0:ROWS_MAX, h, q0:q0 + P], k_st[p][0:ROWS_MAX, h, 0:keys],
                                     start=False, stop=True, skip_group_check=True)
                last.then_inc(s_done, 1)

            def scores_for_exp(b, p, nth, u):
                n = 4 * b + u
                pe.wait_ge(m_in[p][u], 16 * nth)
                wait(pe, exp_done, 2 * n - 1)
                for j in range(HU):
                    h = HU * u + j
                    last = pe.matmul(exp_bank0[:, S * j:S * j + S], k_st[p][0:ROWS_EXP, h, 0:P], q_st[p][0:ROWS_EXP, h, :])
                last.then_inc(st_done, 1)
                wait(pe, exp_done, 2 * n)
                for j in range(HU):
                    h = HU * u + j
                    last = pe.matmul(exp_bank1[:, P * j:P * j + P], k_st[p][0:ROWS_EXP, h, P:S], q_st[p][0:ROWS_EXP, h, P:S])
                last.then_inc(st_done, 1)

            def product_with_v(b, p, u):
                n = 4 * b + u
                r = u % 2
                if u == 0:
                    pe.wait_ge(v_ready, b + 1)
                wait(pe, ot_copied, n - 1)
                pe.wait_ge(sel_done, 2 * n + 1)
                for j in range(HU):
                    pe.matmul(av_bank[r][32 * j:32 * j + 32, :], v_st[p][:, 0, HU * u + j, :], probs[r][:, S * j:S * j + S],
                              start=True, stop=False, skip_group_check=True, tile_position=(0, 32 * j))
                pe.wait_ge(sel_done, 2 * n + 2)
                for j in range(HU):
                    last = pe.matmul(av_bank[r][32 * j:32 * j + 32, P:S], v_st[p][:, 1, HU * u + j, :], probs[r][:, HU * S + P * j:HU * S + P * j + P],
                                     start=False, stop=True, skip_group_check=True, tile_position=(0, 32 * j))
                last.then_inc(av_done, 1)

            def transpose_m(b):
                pe.wait_ge(m_lo, b + 1)
                wait_from_1(pe, res1_done, b - 1)
                for t in range(TB):
                    last = pe.transpose(misc[0:2 * H, P * t:P * t + P], m_split[:, t, :].bitcast(F32), ident[:])
                last.then_inc(mT_done, 1)

            def transpose_o(b, p, t):
                if t == 0:
                    pe.wait_ge(ot_copied, 4 * (b + 1))
                    pe.wait_ge(mT_copied, min(b + 2, B) if isinstance(b, int) else b + 2)
                    wait_from_1(pe, res1_done, b)
                else:
                    wait_from_1(pe, norm_done, 2 * b + 1)
                for u in range(U):
                    last = pe.transpose(misc[:, P * u:P * u + P], o_t[p][:, u, P * t:P * t + P], ident[:])
                last.then_inc(oT_done, 1)

            def transpose_norm(b):
                wait_from_1(pe, norm_done, 2 * b + 2)
                for t in range(TB):
                    last = pe.transpose(misc[:, P * t:P * t + P], o_norm[:, t, :], ident[:])
                last.then_inc(onT_done, 1)

            def project(b):
                pe.wait_ge(onT_copied, b + 1)
                for t in range(TB):
                    last = pe.matmul(misc[:, P * t:P * t + P], o_norm_t[:, P * t:P * t + P], wo[:])
                last.then_inc(proj_done, 1)

            def batch(b, p, nth, first, last):
                def maxima(*ks):
                    if not last:
                        for k in ks:
                            scores_for_max(b + 1, 1 - p, nth + p, k)

                maxima(0, 1)
                scores_for_exp(b, p, nth, 0)
                maxima(2)
                if not first:
                    transpose_o(b - 1, 1 - p, 0)
                maxima(3, 4)
                scores_for_exp(b, p, nth, 1)
                maxima(5)
                if not first:
                    transpose_o(b - 1, 1 - p, 1)
                product_with_v(b, p, 0)
                maxima(6, 7)
                scores_for_exp(b, p, nth, 2)
                if not first:
                    transpose_norm(b - 1)
                maxima(8, 9)
                product_with_v(b, p, 1)
                maxima(10)
                if not first:
                    project(b - 1)
                maxima(11)
                scores_for_exp(b, p, nth, 3)
                product_with_v(b, p, 2)
                if not last:
                    transpose_m(b + 1)
                product_with_v(b, p, 3)

            pe.wait_ge(fw_in, 16 * 19)
            for half in range(2):
                for n in range(4):
                    last = pe.transpose(banks[:, 5 + half, P * n:P * n + P], up_w[:, 4 * half + n, :], ident[:])
                last.then_inc(upT_done, 1)
            pe.transpose(banks[:, 7, 0:2 * E + NS + 1], b_rows[:], ident[0:2 * E + NS + 1, 0:2 * E + NS + 1]).then_inc(bcol_done, 1)
            for half in range(2):
                pe.wait_ge(upT_copied, half + 1)
                for n in range(4):
                    e = 4 * half + n
                    last = pe.matmul(banks[:, 5 + half, P * n:P * n + P], up_t[:, e, :], gate_w[:, min(e, E), :])
                last.then_inc(wg_made, 1)
            pe.wait_ge(bcol_copied, 1)
            for e in range(N):
                col = e if e < E else E + e
                last = pe.matmul(banks[:, 7, e:e + 1], gate_w[:, min(e, E), :], b_cols[:, col:col + 1])
            last.then_inc(bg_made, 1)
            pe.wait_ge(fw_lo, 3)
            pe.wait_ge(gb_ready, 2)
            pe.wait_ge(rw_split, 3)
            pe.wait_ge(const_in, 16 * 6)
            pe.wait_ge(xlo_done, NG)
            pe.wait_ge(qkl_done, 2 * NG)
            pe.wait_ge(v_copied, NG)
            for k in range(NBANK):
                scores_for_max(0, 0, 1, k)
            transpose_m(0)
            batch(0, 0, 1, True, False)
            with pe.Fori(0, B // 2 - 1) as pair:
                batch(2 * pair + 1, 1, pair + 1, False, False)
                batch(2 * pair + 2, 0, pair + 2, False, False)
            batch(B - 1, 1, B // 2, False, True)
            transpose_o(B - 1, 1, 0)
            transpose_o(B - 1, 1, 1)
            transpose_norm(B - 1)
            project(B - 1)

            def three_passes(bank, w_h, w_l, q, done):
                for k, (w, f) in enumerate(((w_h, f_hi), (w_h, f_lo), (w_l, f_hi))):
                    last = pe.matmul(bank, w, f[q][:], start=(k == 0), stop=(k == 2))
                last.then_inc(done, 1)

            def transposes(s, q, src, produced, count):
                pe.wait_ge(produced, count)
                wait_from_1(pe, flo_done, s)
                for t in range(GT):
                    last = pe.transpose(fT_bank[:, P * t:P * t + P], src[:, t, :], ident[:])
                last.then_inc(fT_done, 1)

            def gates(s, q, rnd):
                pe.wait_ge(fhi_done, s + 1)
                wait_from_1(pe, flo_done, s + 1)
                for t in range(GT):
                    for k, (f, w) in enumerate(((f_hi, rout_hi), (f_hi, rout_lo), (f_lo, rout_hi))):
                        last = pe.matmul(rout_bank[:, E * t:E * t + E], f[q][:, P * t:P * t + P], w[:, rnd, :], start=(k == 0), stop=(k == 2))
                last.then_inc(gates_done, 1)

            def weights_t(s):
                pe.wait_ge(rt, ROUTER_STEPS * (s + 1))
                wait_from_1(pe, wT_copied, s)
                for t in range(GT):
                    last = pe.transpose(wT_bank[:, P * t:P * t + P], w_tok_s[:, t, :].bitcast(F32), ident[:])
                last.then_inc(wT_done, 1)

            def down(s, q, tile, w, first, last_one):
                for t in range(GT):
                    last = pe.matmul(down_bank[q][:, P * t:P * t + P], tile[:, P * t:P * t + P], w, start=(first and t == 0), stop=last_one, skip_group_check=True)
                return last

            wait_from_1(pe, res1_done, B)
            pe.wait_ge(exp_done, 8 * B)
            pe.wait_ge(ot_copied, 4 * B)
            transposes(0, 0, x_in[0], xin_ready, 1)
            gates(0, 0, 0)
            weights_t(0)
            with pe.Fori(0, NG // 2) as pair:
                for s, q, rnd in steps_of(pair):
                    next_rnd = rnd if q == 0 else 1 - rnd

                    def down_unit(e):
                        if e < E:
                            wait_from_1(pe, hidw_done, E * s + e + 1)
                            down(s, q, hid_w[e % 2], down_w[:, e, :], False, False).then_inc(down_done, 1)
                        elif e == N - 1:
                            wait_from_1(pe, hsum_done, s + 1)
                            down(s, q, hid_sum, down_w[:, E, :], False, True).then_inc(down_done, 1)

                    for e in range(N):
                        wait_from_1(pe, silu_done, N * s + e)
                        three_passes(gate_bank, gate_hi[:, e, :], gate_lo[:, e, :], q, gate_done)
                        wait_from_1(pe, hid_done, N * s + e)
                        three_passes(up_bank, up_hi[:, e, :], up_lo[:, e, :], q, up_done)
                        if e < E:
                            if e == 0:
                                wait_from_1(pe, wT_copied, s + 1)
                            wait_from_1(pe, hidw_done, E * s + e)
                            pe.matmul(wb_bank, unit_rows_r[:, e, :], w_t[q][0:2 * E, :]).then_inc(wb_done, 1)
                        if e == 0:
                            wait_from_1(pe, ysum_done, s - 1 if q or rnd else s)
                            down(s, q, w_t[q].bitcast(F32), down_b[:], True, False)
                        else:
                            down_unit(e - 1)
                        if e == PREP_T:
                            if rnd == 0 and q == 0:
                                transposes(s + 1, 1, x_in[1], xin_ready, 2 * pair + 2)
                            elif rnd == C - 1 and q == 1:
                                transposes(s + 1, 0, x_in[0], xin_ready, 2 * pair + 3)
                            else:
                                transposes(s + 1, 1 - q, y_out[1 - q], y_done, s)
                        if e == PREP_G:
                            gates(s + 1, 1 - q, next_rnd)
                        if e == PREP_W:
                            weights_t(s + 1)
                    down_unit(N - 1)


_INS = ['L0_attn_x', 'L0_attn_Wq', 'L0_attn_bq', 'L0_attn_Wk', 'L0_attn_Wv', 'L0_attn_Wo', 'L0_attn_bo',
        'L0_ffn_router_W', 'L0_ffn_router_b', 'L0_ffn_gate_bias', 'L0_ffn_exp_Wup', 'L0_ffn_exp_bup', 'L0_ffn_exp_Wg', 'L0_ffn_exp_bg',
        'L0_ffn_exp_Wdown', 'L0_ffn_exp_bdown', 'L0_ffn_share_Wup', 'L0_ffn_share_bup', 'L0_ffn_share_Wg', 'L0_ffn_share_bg',
        'L0_ffn_share_Wdown', 'L0_ffn_share_bdown', 'L0_ffn_norm_w']


def constants():
    import numpy as np
    ident = np.eye(P, dtype=np.float32)
    causal = np.where(np.arange(P)[None, :] > np.arange(P)[:, None], np.float32(-1e30), np.float32(0)).astype(np.float32)
    slopes = (2.0 ** (-8.0 * np.arange(1, H + 1, dtype=np.float32) / H)).astype(np.float32)
    alibi = -(slopes[:, None] * np.arange(S, dtype=np.float32)[None, :]).astype(np.float32)
    hi = (alibi.view(np.uint32) & np.uint32(0xFFFFF000)).view(np.float32)
    of_head = np.zeros((2, H, H, S), np.float32)
    for h in range(H):
        of_head[:, h, h, :] = 1
    rows = np.concatenate([hi[None], (alibi - hi)[None], np.ones((2, H, S), np.float32), of_head.reshape(2 * H, H, S)])
    unit = np.zeros((2, E, E, P), np.float32)
    for e in range(E):
        unit[:, e, e, :] = 1
    before = np.zeros((P, E, E), np.float32)
    before[:] = np.arange(E)[None, :] < np.arange(E)[:, None]
    return {"ident_c": ident, "causal_c": causal, "alibi_c": rows, "unit_c": unit.reshape(2 * E, E * P),
            "before_c": before.reshape(P, E * E)}


def kernel(**inputs):
    import numpy as _np
    import concourse.bacc as _bacc
    from concourse import mybir as _mybir
    from concourse.bass_utils import run_bass_kernel_spmd as _run

    nc = _bacc.Bacc("TRN2", target_bir_lowering=False, num_devices=1)
    arrays, args = {}, []
    for name, a in [(n, inputs[n]) for n in _INS] + list(constants().items()):
        a = _np.ascontiguousarray(a)
        arrays[f"in_{name}_dram"] = a
        args.append(nc.dram_tensor(f"in_{name}_dram", a.shape, _mybir.dt.from_np(a.dtype), kind="ExternalInput").ap())
    args.append(nc.dram_tensor("out_0_dram", (B, S, D), F32, kind="ExternalOutput").ap())
    program(nc, *args)
    r = _run(nc, [arrays], core_ids=[0])
    return r.results[0]["out_0_dram"]
```

```python
from contextlib import ExitStack

import concourse.bass as bass
from concourse import mybir

F32 = mybir.dt.float32
F32R = mybir.dt.float32r
BF16 = mybir.dt.bfloat16
ALU = mybir.AluOpType
ACT = mybir.ActivationFunctionType
AX = mybir.AxisListType

P = 128
B, S, D = 8, 256, 128
H, HD = 16, 8
TB = S // P
NT = B * TB
GT = 4
NG = NT // GT
GW = GT * P
U = 4
HU = H // U
NBANK = 3 * U
ROWS_QK = 3 * HD
ROWS_MAX = 96
ROWS_EXP = 128
QSCALE = float(HD) ** -0.5
LN_EPS = 1e-5
C, E, TOPK = 2, 6, 2
NS = 2
N = E + NS
FF_EPS = 1e-6
ROUTER_STEPS = 14
ROUTER_FIRST = 5


def program(nc, x, Wq, bq, Wk, Wv, Wo, bo, router_W, router_b, gate_bias, exp_Wup, exp_bup, exp_Wg, exp_bg,
            exp_Wdown, exp_bdown, share_Wup, share_bup, share_Wg, share_bg, share_Wdown, share_bdown, norm_w,
            ident_c, causal_c, alibi_c, unit_c, before_c, out):
    ctx = ExitStack()
    with ctx:
        def sb(name, shape, dt=F32):
            return ctx.enter_context(nc.sbuf_tensor(name, shape, dt))

        def sem(name):
            return ctx.enter_context(nc.semaphore(name))

        banks = ctx.enter_context(nc.psum_tensor("banks", [P, 8, 512], F32))

        ident = sb("ident", [P, P])
        ident_bf = sb("ident_bf", [P, P], BF16)
        causal = sb("causal", [P, P])
        step = sb("step", [1, 2])
        causal_bf = sb("causal_bf", [P, 4, P], BF16)
        w_in = sb("w_in", [P, 3, P])
        wqs = sb("wqs", [P, P])
        w_hi = sb("w_hi", [P, 3, P], F32R)
        w_lo = sb("w_lo", [P, 3, P], F32R)
        wo = sb("wo", [P, P])
        bo_all = sb("bo_all", [P, P])
        bq_row = sb("bq_row", [1, P])
        bq_perm = sb("bq_perm", [1, P])
        scale_one = sb("scale_one", [1, 1])
        bq_col = sb("bq_col", [P, 1])
        minus_half = sb("minus_half", [P, GT])

        x_sb = sb("x_sb", [P, NT, D])
        xb_sb = sb("xb_sb", [P, NT, D])
        v_sb = sb("v_sb", [P, NT, D])
        x1 = sb("x1", [P, NT, D])
        xT_hi = sb("xT_hi", [P, 2, GW], F32R)
        xT_lo = sb("xT_lo", [P, 2, GW], F32R)
        q_hi = sb("q_hi", [P, 2, GW], F32R)
        q_lo = sb("q_lo", [P, 2, GW], F32R)
        k_hi = sb("k_hi", [P, 2, GW], F32R)
        k_lo = sb("k_lo", [P, 2, GW], F32R)

        up_w = sb("up_w", [P, N, P])
        gate_w = sb("gate_w", [P, E + 1, P])
        up_t = sb("up_t", [P, N, P])
        down_w = sb("down_w", [P, E + 1, P])
        up_hi = sb("up_hi", [P, N, P], F32R)
        up_lo = sb("up_lo", [P, N, P], F32R)
        gate_hi = sb("gate_hi", [P, N, P], F32R)
        gate_lo = sb("gate_lo", [P, N, P], F32R)
        down_b = sb("down_b", [2 * E + 1, P])
        b_rows = sb("b_rows", [2 * E + NS + 1, P])
        b_cols = sb("b_cols", [P, 2 * E + NS + 1])
        gate_b = sb("gate_b", [P, N])
        unit_rows = sb("unit_rows", [2 * E, E * P])
        unit_rows_r = sb("unit_rows_r", [2 * E, E, P], F32R)
        before = sb("before", [P, E * E])
        rout_w = sb("rout_w", [P, C, E])
        rout_hi = sb("rout_hi", [P, C, E], F32R)
        rout_lo = sb("rout_lo", [P, C, E], F32R)
        rout_b = sb("rout_b", [P, C, E])
        rout_gb = sb("rout_gb", [P, C, E])
        norm_all = sb("norm_all", [P, C, D])

        attention = ExitStack()

        def sba(name, shape, dt=F32):
            return attention.enter_context(nc.sbuf_tensor(name, shape, dt))

        q_st = [sba(f"q_st{p}", [P, H, S], F32R) for p in range(2)]
        k_st = [sba(f"k_st{p}", [P, H, S], F32R) for p in range(2)]
        v_st = [sba(f"v_st{p}", [P, TB, H, 32]) for p in range(2)]
        m_neg = sba("m_neg", [P, TB, H])
        m_split = sba("m_split", [P, TB, 2 * H], F32R)
        m_rows = sba("m_rows", [2 * H, S], F32R)
        probs = [sba(f"probs{r}", [P, HU * S + HU * P]) for r in range(2)]
        o_t = [sba(f"o_t{p}", [P, U, S]) for p in range(2)]
        den_inv = sba("den_inv", [P, H])
        o_norm = sba("o_norm", [P, TB, D])
        o_norm_t = sba("o_norm_t", [P, S])
        res1 = sba("res1", [P, TB, D])
        stats1 = sba("stats1", [P, TB, 6])
        mv1 = sba("mv1", [P, TB, 2])
        var1 = sba("var1", [P, TB])
        rstd1 = sba("rstd1", [P, TB])

        attention.close()
        x_in = [sb(f"x_in{q}", [P, GT, D]) for q in range(2)]
        y_out = [sb(f"y_out{q}", [P, GT, D]) for q in range(2)]
        y_sum = [sb(f"y_sum{q}", [P, GT, D]) for q in range(2)]
        y_end = [sb(f"y_end{q}", [P, GT, D]) for q in range(2)]
        x_end = [sb(f"x_end{q}", [P, GT, D]) for q in range(2)]
        f_hi = [sb(f"f_hi{q}", [P, GW], F32R) for q in range(2)]
        f_lo = [sb(f"f_lo{q}", [P, GW], F32R) for q in range(2)]
        silu = [sb(f"silu{r}", [P, GW]) for r in range(2)]
        wb_sb = [sb(f"wb_sb{r}", [P, GW]) for r in range(2)]
        silu_w = [sb(f"silu_w{r}", [P, GW]) for r in range(2)]
        hid_w = [sb(f"hid_w{r}", [P, GW]) for r in range(2)]
        hid_s = [sb(f"hid_s{r}", [P, GW]) for r in range(2)]
        hid_sum = sb("hid_sum", [P, GW])
        squares = sb("squares", [P, GT, D])
        g_val = sb("g_val", [P, GT, E])
        g_bias = sb("g_bias", [P, GT, E])
        beats = sb("beats", [P, GT, E, E])
        ties = sb("ties", [P, GT, E, E])
        rank = sb("rank", [P, GT, E])
        half_sel = sb("half_sel", [P, GT, E])
        sel_g = sb("sel_g", [P, GT, E])
        half_sum = sb("half_sum", [P, GT])
        g_diff = sb("g_diff", [P, GT, E])
        g_tanh = sb("g_tanh", [P, GT, E])
        w_tok = sb("w_tok", [P, GT, E])
        w_tok_s = sb("w_tok_s", [P, GT, 2 * E], F32R)
        w_t = [sb(f"w_t{q}", [2 * E + 1, GW], F32R) for q in range(2)]
        ssq = sb("ssq", [P, GT])
        ms = sb("ms", [P, GT])
        rms_inv = sb("rms_inv", [P, GT])
        stats2 = sb("stats2", [P, GT, 6])
        mv2 = sb("mv2", [P, GT, 2])
        var2 = sb("var2", [P, GT])
        rstd2 = sb("rstd2", [P, GT])

        q_rows = nc.dram_tensor("q_rows", [3, HD * H, B * S], F32, kind="Internal").ap()
        const_rows = nc.dram_tensor("const_rows", [4 + 2 * H, H, S], F32, kind="Internal").ap()
        k_rows = nc.dram_tensor("k_rows", [3, HD * H, B * S], F32, kind="Internal").ap()

        x_loaded = [sem(f"x_loaded{g}") for g in range(NG)]
        w_loaded = sem("w_loaded")
        c_loaded = sem("c_loaded")
        cast_done = sem("cast_done")
        w_split = sem("w_split")
        bq_cols = sem("bq_cols")
        bq_made = sem("bq_made")
        bq_ready = sem("bq_ready")
        ones_ready = sem("ones_ready")
        xb_ready = sem("xb_ready")
        st_zero = sem("st_zero")
        const_copied = sem("const_copied")
        const_in = sem("const_in")
        xT_done = sem("xT_done")
        xhi_done = sem("xhi_done")
        xlo_done = sem("xlo_done")
        qkv_done = sem("qkv_done")
        qkh_done = sem("qkh_done")
        qkl_done = sem("qkl_done")
        v_copied = sem("v_copied")
        rows_out = [sem(f"rows_out{g}") for g in range(NG)]
        st_in = [[sem(f"st_in{p}{u}") for u in range(U)] for p in range(2)]
        s_done = sem("s_done")
        max_done = sem("max_done")
        m_hi = sem("m_hi")
        m_lo = sem("m_lo")
        mT_done = sem("mT_done")
        mT_copied = sem("mT_copied")
        m_in = [[sem(f"m_in{p}{u}") for u in range(U)] for p in range(2)]
        st_done = sem("st_done")
        exp_done = sem("exp_done")
        sel_done = sem("sel_done")
        step_done = sem("step_done")
        v_ready = sem("v_ready")
        v_const = sem("v_const")
        av_done = sem("av_done")
        ot_copied = sem("ot_copied")
        oT_done = sem("oT_done")
        den_done = sem("den_done")
        norm_done = sem("norm_done")
        onT_done = sem("onT_done")
        onT_copied = sem("onT_copied")
        proj_done = sem("proj_done")
        res1_done = sem("res1_done")
        bn1_done = sem("bn1_done")
        mv1_done = sem("mv1_done")
        var1_done = sem("var1_done")
        rstd1_done = sem("rstd1_done")
        x1_done = sem("x1_done")
        out_done = [sem(f"out_done{q}") for q in range(2)]
        fw_in = sem("fw_in")
        upT_done = sem("upT_done")
        upT_copied = sem("upT_copied")
        wg_made = sem("wg_made")
        fw_hi = sem("fw_hi")
        fw_lo = sem("fw_lo")
        bcol_done = sem("bcol_done")
        bcol_copied = sem("bcol_copied")
        bg_made = sem("bg_made")
        gb_ready = sem("gb_ready")
        rw_split = sem("rw_split")
        wt_ready = sem("wt_ready")
        xin_ready = sem("xin_ready")
        fT_done = sem("fT_done")
        fhi_done = sem("fhi_done")
        flo_done = sem("flo_done")
        gates_done = sem("gates_done")
        rt = sem("rt")
        tanh_done = sem("tanh_done")
        wtok_done = sem("wtok_done")
        wT_done = sem("wT_done")
        wT_copied = sem("wT_copied")
        gate_done = sem("gate_done")
        up_done = sem("up_done")
        wb_done = sem("wb_done")
        silu_done = sem("silu_done")
        hid_done = sem("hid_done")
        wb_copied = sem("wb_copied")
        silu_w_done = sem("silu_w_done")
        hsum_done = sem("hsum_done")
        down_done = sem("down_done")
        ysum_done = sem("ysum_done")
        ssq_done = sem("ssq_done")
        ms_done = sem("ms_done")
        rms_done = sem("rms_done")
        y_done = sem("y_done")
        xend_done = sem("xend_done")
        bn2_done = sem("bn2_done")
        mv2_done = sem("mv2_done")
        var2_done = sem("var2_done")
        rstd2_done = sem("rstd2_done")
        o_ready = sem("o_ready")

        def wait(eng, s, value):
            if not isinstance(value, int) or value > 0:
                eng.wait_ge(s, value)

        from_1 = {"pe": (oT_done, onT_done, proj_done, av_done, down_done),
                  "dve": (res1_done, norm_done, x1_done, hid_done, ms_done, xend_done, bn2_done, var2_done, ysum_done, flo_done),
                  "act": (silu_done, wT_copied, wb_copied),
                  "pool": (rstd1_done, silu_w_done)}

        def wait_from_1(eng, s, value):
            if not isinstance(value, int) or value > 0:
                eng.wait_ge(s, value + 1)

        def start_from_1(eng, name):
            for s in from_1[name]:
                eng.sem_inc(s, 1)

        max_bank = [banks[:, 0, :], banks[:, 1, :]]
        exp_bank0 = banks[:, 2:4, :].rearrange("p a c -> p (a c)")
        exp_bank1 = banks[:, 4, :]
        av_bank = [banks[:, 5, 0:S], banks[:, 6, 0:S]]
        misc = banks[:, 7, :]

        gate_bank, up_bank, wb_bank, fT_bank = (banks[:, n, :] for n in range(4))
        rout_bank, wT_bank = banks[:, 4, 0:GT * E], banks[0:2 * E, 5, :]
        down_bank = [banks[:, 6, :], banks[:, 7, :]]

        def steps_of(pair):
            return [(4 * pair + n, n % 2, n // 2) for n in range(4)]

        def weights_of(u):
            return E + u if u < NS else u - NS

        block = ctx.enter_context(nc.Block())

        @block.sync
        def _(sp):
            x_tiles = x.rearrange("b (u p) d -> p (b u) d", p=P)
            for g in range(NG):
                sp.dma_start(x_sb[:, GT * g:GT * g + GT, :], x_tiles[:, GT * g:GT * g + GT, :]).then_inc(x_loaded[g], 16)
            sp.dma_start(bo_all[:], bo.rearrange("(o d) -> o d", o=1).broadcast_to((P, D))).then_inc(c_loaded, 16)
            sp.dma_start(wo[:], Wo).then_inc(c_loaded, 16)
            sp.dma_start(up_w[:, 0:E, :], exp_Wup.rearrange("e h i -> h e i")).then_inc(fw_in, 16)
            sp.dma_start(up_w[:, E:N, :], share_Wup.rearrange("h (s i) -> h s i", s=NS)).then_inc(fw_in, 16)
            sp.dma_start(gate_w[:, 0:E, :], exp_Wg.rearrange("e h i -> h e i")).then_inc(fw_in, 16)
            sp.dma_start(gate_w[:, E, :], share_Wg).then_inc(fw_in, 16)
            sp.dma_start(down_w[:, 0:E, :], exp_Wdown.rearrange("e h i -> h e i")).then_inc(fw_in, 16)
            sp.dma_start(down_w[:, E, :], share_Wdown).then_inc(fw_in, 16)
            for n in range(2):
                sp.dma_start(down_b[E * n:E * n + E, :], exp_bdown).then_inc(fw_in, 16)
            sp.dma_start(down_b[2 * E:2 * E + 1, :], share_bdown.rearrange("(o d) -> o d", o=1)).then_inc(fw_in, 16)
            sp.dma_start(b_rows[0:E, :], exp_bup).then_inc(fw_in, 16)
            sp.dma_start(b_rows[E:2 * E, :], exp_bg).then_inc(fw_in, 16)
            sp.dma_start(b_rows[2 * E:2 * E + NS, :], share_bup.rearrange("(s d) -> s d", s=NS)).then_inc(fw_in, 16)
            sp.dma_start(b_rows[2 * E + NS:2 * E + NS + 1, :], share_bg.rearrange("(o d) -> o d", o=1)).then_inc(fw_in, 16)
            sp.dma_start(unit_rows[:], unit_c).then_inc(fw_in, 16)
            sp.dma_start(before[:], before_c).then_inc(fw_in, 16)
            sp.dma_start(rout_w[:], router_W.rearrange("c h e -> h c e")).then_inc(fw_in, 16)
            for dst, src in ((rout_b, router_b), (rout_gb, gate_bias), (norm_all, norm_w)):
                sp.dma_start(dst[:], src.rearrange("(o c) e -> o c e", o=1).broadcast_to((P, C, src.shape[1]))).then_inc(fw_in, 16)

            def rows_to_dram(g):
                sp.wait_ge(qkh_done, 2 * g + 2)
                sp.wait_ge(qkl_done, 2 * g + 2)
                for dst, parts in ((q_rows, (q_hi, q_hi, q_lo)), (k_rows, (k_hi, k_lo, k_hi))):
                    for n, part in enumerate(parts):
                        sp.dma_start(dst[n, :, g * GW:(g + 1) * GW], part[:, g % 2, :].bitcast(F32)).then_inc(rows_out[g], 16)

            def stacks_in(b, p, u):
                for dst, src in ((q_st, q_rows), (k_st, k_rows)):
                    sp.dma_start(dst[p][0:24, HU * u:HU * (u + 1), :].bitcast(F32),
                                 src[:, :, bass.ds(b * S, S)].rearrange("n (d h) t -> (n d) h t", h=H)[:, HU * u:HU * (u + 1), :]
                                 ).then_inc(st_in[p][u], 16)

            rows_to_dram(0)
            sp.wait_ge(rows_out[0], 96)
            sp.wait_ge(st_zero, 4)
            for b in range(2):
                for u in range(U):
                    stacks_in(b, b, u)
            for g in range(1, NG):
                rows_to_dram(g)
            for g in range(1, NG):
                sp.wait_ge(rows_out[g], 96)
            with sp.Fori(1, B // 2) as pair:
                for p in range(2):
                    for u in range(U):
                        sp.wait_ge(st_done, 8 * (2 * pair + p - 2) + 2 * u + 2)
                        stacks_in(2 * pair + p, p, u)
            out_tiles = out.rearrange("b (u p) d -> p (b u) d", p=P)
            with sp.Fori(0, NG // 2) as pair:
                for q in range(2):
                    sp.wait_ge(o_ready, 2 * pair + q + 1)
                    sp.dma_start(out_tiles[:, bass.ds((2 * pair + q) * GT, GT), :], xb_sb[:, bass.ds((2 * pair + q) * GT, GT), :]).then_inc(out_done[q], 16)
            for q in range(2):
                sp.wait_ge(out_done[q], 16 * (NG // 2))

        @block.gpsimd
        def _(pool):
            start_from_1(pool, "pool")
            for st in (q_st[0], k_st[0]):
                pool.memset(st[:].bitcast(F32), 0.0).then_inc(st_zero, 1)
            for p in range(2):
                pool.memset(v_st[p][:], 0.0).then_inc(v_const, 1)
            pool.wait_ge(v_const, 2)
            for p in range(2):
                pool.memset(v_st[p][:, :, :, HD:HD + 1], 1.0).then_inc(v_const, 1)
            pool.memset(minus_half[:], -0.5).then_inc(ones_ready, 1)
            pool.memset(step[:], 1.0).then_inc(ones_ready, 1)
            pool.wait_ge(ones_ready, 2)
            pool.memset(scale_one[:], QSCALE).then_inc(ones_ready, 1)
            pool.wait_ge(v_const, 4)
            pool.wait_ge(c_loaded, 16 * 5)
            for g in range(NG):
                pool.wait_ge(x_loaded[g], 16)
                pool.tensor_tensor(xb_sb[:, GT * g:GT * g + GT, :], x_sb[:, GT * g:GT * g + GT, :],
                                   bo_all[:].rearrange("p (o d) -> p o d", o=1).broadcast_to((P, GT, D)), ALU.add).then_inc(xb_ready, 1)

            def stage_v(b, p):
                wait_from_1(pool, av_done, 4 * (b - 1))
                pool.tensor_copy(v_st[p][:, :, :, 0:HD], v_sb[:, bass.ds(b * TB, TB), :].rearrange("p t (h d) -> p t h d", h=H)).then_inc(v_ready, 1)

            def causal_select(n, r, half):
                pool.wait_ge(exp_done, 2 * n + half + 1)
                wait(pool, step_done, 2 * n + half)
                pool.tensor_tensor(step[:, 1:2], step[:, 0:1], step[:, 0:1], ALU.mult).then_inc(step_done, 1)
                v = probs[r][:, half * HU * S:half * HU * S + HU * (P if half else S)].rearrange("p (h q) -> p h q", h=HU)[:, :, 0:P]
                pool.affine_select(out=v, in_=v, compare_op=ALU.is_ge, fill=0.0, base=0,
                                   pattern=[[0, HU], [1, P]], channel_multiplier=-1).then_inc(sel_done, 1)

            def rstd(b):
                pool.wait_ge(var1_done, b + 1)
                pool.tensor_tensor(rstd1[:], var1[:], minus_half[:, 0:TB], ALU.pow).then_inc(rstd1_done, 1)

            def batch(b, p, first, last):
                for u in range(U):
                    for half in range(2):
                        causal_select(4 * b + u, u % 2, half)
                    if u == 1 and not last:
                        stage_v(b + 1, 1 - p)
                if not first:
                    rstd(b - 1)

            pool.wait_ge(v_copied, 1)
            stage_v(0, 0)
            pool.wait_ge(v_copied, NG)
            batch(0, 0, True, False)
            with pool.Fori(0, B // 2 - 1) as pair:
                batch(2 * pair + 1, 1, False, False)
                batch(2 * pair + 2, 0, False, False)
            batch(B - 1, 1, False, True)
            rstd(B - 1)

            def stage_x(group, q):
                pool.tensor_copy(x_in[q][:], x1[:, bass.ds(group * GT, GT), :]).then_inc(xin_ready, 1)

            def power(dst, src, produced, count, done):
                wait_from_1(pool, produced, count)
                pool.tensor_tensor(dst[:], src[:], minus_half[:], ALU.pow).then_inc(done, 1)

            wait_from_1(pool, x1_done, B)
            wait_from_1(pool, av_done, 4 * B)
            wait_from_1(pool, oT_done, 2 * B)
            wait_from_1(pool, proj_done, B)
            for q in range(2):
                pool.memset(w_t[q][:].bitcast(F32), 2.0).then_inc(wt_ready, 1)
            for q in range(2):
                stage_x(q, q)
            with pool.Fori(0, NG // 2) as pair:
                def rms(s):
                    power(rms_inv, ms, ms_done, s + 1, rms_done)

                def rstd_end(q):
                    power(rstd2, var2, var2_done, 2 * pair + q + 1, rstd2_done)

                steps = steps_of(pair)
                for n, (s, q, rnd) in enumerate(steps):
                    wait_from_1(pool, hid_done, N * s + NS)
                    pool.tensor_tensor(hid_sum[:], hid_s[0][:], hid_s[1][:], ALU.add).then_inc(hsum_done, 1)
                    for e in range(E):
                        wait_from_1(pool, silu_done, N * s + NS + e + 1)
                        wait_from_1(pool, wb_copied, E * s + e + 1)
                        if e >= 2:
                            wait_from_1(pool, hid_done, N * s + NS + e - 1)
                        pool.tensor_tensor(silu_w[e % 2][:], silu[e % 2][:], wb_sb[e % 2][:], ALU.mult).then_inc(silu_w_done, 1)
                        if e == 0 and n:
                            rms(s - 1)
                        if e == 4 and n and steps[n - 1][2] == C - 1:
                            rstd_end(steps[n - 1][1])
                        if e == 5 and n in (1, 2):
                            stage_x((2 * pair + 1 + n) % NG, n - 1)
                rms(4 * pair + 3)
                rstd_end(1)

        @block.scalar
        def _(act):
            start_from_1(act, "act")
            for n, w in enumerate((Wq, Wk, Wv)):
                act.dma_start(w_in[:, n, :], w).then_inc(w_loaded, 16)
            act.dma_start(ident[:], ident_c).then_inc(c_loaded, 16)
            act.dma_start(causal[:], causal_c).then_inc(c_loaded, 16)
            act.dma_start(bq_row[:], bq.rearrange("(o d) -> o d", o=1)).then_inc(c_loaded, 16)
            act.dma_start(const_rows, alibi_c).then_inc(const_copied, 16)
            act.wait_ge(bq_made, 1)
            act.copy(bq_col[:], banks[:, 7, 0:1]).then_inc(bq_ready, 1)
            act.wait_ge(bq_ready, 1)
            for g in range(NG):
                act.wait_ge(xT_done, g + 1)
                wait(act, qkv_done, 3 * (g - 1))
                act.copy(xT_hi[:, g % 2, :], banks[:, g % 2, :]).then_inc(xhi_done, 1)
                if g >= 2:
                    act.wait_ge(rows_out[g - 2], 96)
                act.wait_ge(qkv_done, 3 * g + 1)
                act.activation(q_hi[:, g % 2, :], banks[:, 2, :], ACT.Identity, bias=bq_col[:]).then_inc(qkh_done, 1)
                act.wait_ge(qkv_done, 3 * g + 2)
                act.copy(k_hi[:, g % 2, :], banks[:, 3, :]).then_inc(qkh_done, 1)
                act.wait_ge(qkv_done, 3 * g + 3)
                act.copy(v_sb[:, GT * g:GT * g + GT, :].rearrange("p t d -> p (t d)"), banks[:, 4, :]).then_inc(v_copied, 1)
                if g == 0:
                    act.wait_ge(const_copied, 16)
                    act.wait_ge(st_zero, 4)
                    for p in range(2):
                        act.dma_start(k_st[p][24:26, :, :].bitcast(F32), const_rows[0:2]).then_inc(const_in, 16)
                        act.dma_start(q_st[p][24:26, :, :].bitcast(F32), const_rows[2:4]).then_inc(const_in, 16)
                        act.dma_start(k_st[p][ROWS_MAX:ROWS_EXP, :, :].bitcast(F32), const_rows[4:4 + 2 * H]).then_inc(const_in, 16)

            for half in range(2):
                act.wait_ge(upT_done, half + 1)
                act.copy(up_t[:, 4 * half:4 * half + 4, :].rearrange("p n i -> p (n i)"), banks[:, 5 + half, :]).then_inc(upT_copied, 1)
            act.wait_ge(bcol_done, 1)
            act.copy(b_cols[:], banks[:, 7, 0:2 * E + NS + 1]).then_inc(bcol_copied, 1)
            act.wait_ge(fw_in, 16 * 19)
            act.copy(up_hi[:], up_w[:]).then_inc(fw_hi, 1)
            for half in range(2):
                act.wait_ge(wg_made, half + 1)
                act.copy(gate_hi[:, 4 * half:4 * half + 4, :].rearrange("p n i -> p (n i)"), banks[:, 5 + half, :]).then_inc(fw_hi, 1)

            def exps(n, r):
                for half, bank, lo, w in ((0, exp_bank0, 0, HU * S), (1, exp_bank1, HU * S, HU * P)):
                    act.wait_ge(st_done, 2 * n + half + 1)
                    if not half:
                        wait_from_1(act, av_done, n - 1)
                    act.activation(probs[r][:, lo:lo + w], bank, ACT.Exp).then_inc(exp_done, 1)

            def copy_av(b, p, u):
                n = 4 * b + u
                wait_from_1(act, av_done, n + 1)
                if u == 0:
                    wait_from_1(act, oT_done, 2 * (b - 1))
                act.copy(o_t[p][:, u, :], av_bank[u % 2]).then_inc(ot_copied, 1)

            def m_rows_in(b, p, before):
                act.wait_ge(mT_done, b + 1)
                for u in range(U):
                    wait(act, m_in[1 - p][u], 16 * before)
                act.copy(m_rows[:], misc[0:2 * H, 0:S]).then_inc(mT_copied, 1)
                act.wait_ge(mT_copied, b + 1)
                wait(act, st_done, 8 * (b - 1))
                for u in range(U):
                    act.dma_start(q_st[p][ROWS_MAX:ROWS_EXP, HU * u:HU * (u + 1), :].bitcast(F32),
                                  m_rows[:].bitcast(F32).rearrange("r (o t) -> r o t", o=1).broadcast_to((2 * H, HU, S))).then_inc(m_in[p][u], 16)

            def batch(b, p, nth, first, last):
                if not first:
                    copy_av(b - 1, 1 - p, 3)
                exps(4 * b, 0)
                exps(4 * b + 1, 1)
                copy_av(b, p, 0)
                exps(4 * b + 2, 0)
                if not first:
                    copy_onT(b - 1)
                copy_av(b, p, 1)
                exps(4 * b + 3, 1)
                copy_av(b, p, 2)
                if not last:
                    m_rows_in(b + 1, 1 - p, nth)

            def copy_onT(b):
                wait_from_1(act, onT_done, b + 1)
                wait_from_1(act, proj_done, b)
                act.copy(o_norm_t[:], misc[:, 0:S]).then_inc(onT_copied, 1)

            m_rows_in(0, 0, 0)
            batch(0, 0, 1, True, False)
            with act.Fori(0, B // 2 - 1) as pair:
                batch(2 * pair + 1, 1, pair + 1, False, False)
                batch(2 * pair + 2, 0, pair + 2, False, False)
            batch(B - 1, 1, B // 2, False, True)
            copy_av(B - 1, 1, 3)
            copy_onT(B - 1)

            def high_part(s, q):
                act.wait_ge(fT_done, s + 1)
                act.copy(f_hi[q][:], fT_bank).then_inc(fhi_done, 1)

            def router_tanh(s):
                act.wait_ge(rt, ROUTER_STEPS * s + ROUTER_STEPS - 3)
                act.activation(g_tanh[:], g_diff[:], ACT.Tanh).then_inc(tanh_done, 1)

            def weights_t(s, q):
                act.wait_ge(wT_done, s + 1)
                act.copy(w_t[q][0:2 * E, :], wT_bank).then_inc(wT_copied, 1)

            def squares_of(s, q):
                wait_from_1(act, ysum_done, s + 1)
                wait_from_1(act, ms_done, s)
                for t in range(GT):
                    last = act.activation(squares[:, t, :], y_sum[q][:, t, :], ACT.Square, accum_out=ssq[:, t:t + 1])
                last.then_inc(ssq_done, 1)

            act.wait_ge(xin_ready, 1)
            high_part(0, 0)
            act.wait_ge(wt_ready, 2)
            with act.Fori(0, NG // 2) as pair:
                for n, (s, q, rnd) in enumerate(steps_of(pair)):
                    for u in range(N):
                        r = u % 2
                        if u >= NS:
                            e = u - NS
                            act.wait_ge(wb_done, E * s + e + 1)
                            if e >= 2:
                                wait_from_1(act, silu_w_done, E * s + e - 1)
                            act.copy(wb_sb[r][:], wb_bank).then_inc(wb_copied, 1)
                        act.wait_ge(gate_done, N * s + u + 1)
                        if u == 1:
                            wait_from_1(act, silu_w_done, E * s)
                        elif NS <= u < NS + 2:
                            wait_from_1(act, hid_done, N * s + u - 1)
                        act.activation(silu[r][:], gate_bank, ACT.Silu, bias=gate_b[:, weights_of(u):weights_of(u) + 1]).then_inc(silu_done, 1)
                        if u == 0:
                            router_tanh(s)
                        if u == 1:
                            weights_t(s, q)
                        if u == 2 and n:
                            squares_of(s - 1, 1 - q)
                        if u == 5:
                            high_part(s + 1, 1 - q)
                squares_of(4 * pair + 3, 1)

        @block.vector
        def _(dve):
            start_from_1(dve, "dve")
            for st in (q_st[1], k_st[1]):
                dve.memset(st[:].bitcast(F32), 0.0).then_inc(st_zero, 1)
            dve.wait_ge(c_loaded, 16 * 5)
            dve.tensor_copy(bq_perm[:].rearrange("o (d h) -> o d h", h=H), bq_row[:].rearrange("o (h d) -> o d h", h=H)).then_inc(bq_cols, 1)
            dve.tensor_copy(ident_bf[:], ident[:]).then_inc(cast_done, 1)
            dve.tensor_copy(causal_bf[:], causal[:].rearrange("p (o d) -> p o d", o=1).broadcast_to((P, 4, P))).then_inc(cast_done, 1)
            dve.wait_ge(w_loaded, 48)
            dve.tensor_scalar(wqs[:], w_in[:, 0, :], QSCALE, None, ALU.mult).then_inc(cast_done, 1)
            dve.wait_ge(cast_done, 3)
            def cols(w, n):
                return w if n == 2 else w.rearrange("p (h d) -> p d h", h=H)

            def as_cols(w, n):
                return w if n == 2 else w.rearrange("p (d h) -> p d h", h=H)
            for n in range(3):
                src = wqs[:] if n == 0 else w_in[:, n, :]
                dve.tensor_copy(as_cols(w_hi[:, n, :], n), cols(src, n)).then_inc(w_split, 1)
                dve.wait_ge(w_split, 2 * n + 1)
                dve.tensor_tensor(as_cols(w_lo[:, n, :], n), cols(src, n), as_cols(w_hi[:, n, :].bitcast(F32), n), ALU.subtract).then_inc(w_split, 1)
            dve.wait_ge(bq_ready, 1)
            for g in range(NG):
                dve.wait_ge(xhi_done, g + 1)
                dve.tensor_tensor(xT_lo[:, g % 2, :], banks[:, g % 2, :], xT_hi[:, g % 2, :].bitcast(F32), ALU.subtract).then_inc(xlo_done, 1)
                dve.wait_ge(qkh_done, 2 * g + 1)
                if g >= 2:
                    dve.wait_ge(rows_out[g - 2], 96)
                dve.scalar_tensor_tensor(out=q_lo[:, g % 2, :], in0=banks[:, 2, :], scalar=bq_col[:], in1=q_hi[:, g % 2, :].bitcast(F32),
                                         op0=ALU.add, op1=ALU.subtract).then_inc(qkl_done, 1)
                dve.wait_ge(qkh_done, 2 * g + 2)
                dve.tensor_tensor(k_lo[:, g % 2, :], banks[:, 3, :], k_hi[:, g % 2, :].bitcast(F32), ALU.subtract).then_inc(qkl_done, 1)

            dve.wait_ge(fw_in, 16 * 19)
            dve.tensor_copy(unit_rows_r[:], unit_rows[:].rearrange("p (e i) -> p e i", e=E)).then_inc(rw_split, 1)
            dve.tensor_copy(rout_hi[:], rout_w[:]).then_inc(rw_split, 1)
            dve.wait_ge(rw_split, 2)
            dve.tensor_tensor(rout_lo[:], rout_w[:], rout_hi[:].bitcast(F32), ALU.subtract).then_inc(rw_split, 1)
            dve.wait_ge(fw_hi, 1)
            dve.tensor_tensor(up_lo[:], up_w[:], up_hi[:].bitcast(F32), ALU.subtract).then_inc(fw_lo, 1)
            for half in range(2):
                dve.wait_ge(fw_hi, 2 + half)
                dve.tensor_tensor(gate_lo[:, 4 * half:4 * half + 4, :].rearrange("p n i -> p (n i)"), banks[:, 5 + half, :],
                                  gate_hi[:, 4 * half:4 * half + 4, :].rearrange("p n i -> p (n i)").bitcast(F32), ALU.subtract).then_inc(fw_lo, 1)
            dve.wait_ge(bg_made, 1)
            dve.tensor_tensor(gate_b[:, 0:E], banks[:, 7, 0:E], b_cols[:, E:2 * E], ALU.add).then_inc(gb_ready, 1)
            dve.tensor_scalar(gate_b[:, E:N], banks[:, 7, E:N], b_cols[:, 2 * E + NS:2 * E + NS + 1], None, ALU.add).then_inc(gb_ready, 1)

            def maxima(b, k):
                u, part = divmod(k, 3)
                dve.wait_ge(s_done, NBANK * b + k + 1)
                if k == 0:
                    wait(dve, m_lo, b)
                if part == 0:
                    dst, heads = m_neg[:, 0, HU * u:HU * u + HU], HU
                else:
                    h0 = HU * u + 2 * (part - 1)
                    dst, heads = m_neg[:, 1, h0:h0 + 2], 2
                dve.tensor_reduce(dst, max_bank[k % 2].rearrange("p (h k) -> p h k", h=heads), AX.X, ALU.max, negate=True).then_inc(max_done, 1)

            def split_m(b):
                dve.wait_ge(max_done, NBANK * (b + 1))
                wait(dve, mT_done, b)
                dve.tensor_copy(m_split[:, :, 0:H], m_neg[:]).then_inc(m_hi, 1)
                dve.wait_ge(m_hi, b + 1)
                dve.tensor_tensor(m_split[:, :, H:2 * H], m_neg[:], m_split[:, :, 0:H].bitcast(F32), ALU.subtract).then_inc(m_lo, 1)

            def normalise(b, t):
                wait_from_1(dve, oT_done, 2 * b + t + 1)
                o = misc.rearrange("p (h c) -> p h c", h=H)
                wait_from_1(dve, norm_done, 2 * b + t)
                dve.reciprocal(den_inv[:], o[:, :, HD]).then_inc(den_done, 1)
                dve.wait_ge(den_done, 2 * b + t + 1)
                if t == 0:
                    wait_from_1(dve, onT_done, b)
                dve.tensor_tensor(o_norm[:, t, :].rearrange("p (h d) -> p h d", h=H), o[:, :, 0:HD],
                                  den_inv[:].rearrange("p (h o) -> p h o", o=1).broadcast_to((P, H, HD)), ALU.mult).then_inc(norm_done, 1)

            def residual(b):
                wait_from_1(dve, proj_done, b + 1)
                wait_from_1(dve, x1_done, b)
                dve.tensor_tensor(res1[:], misc[:, 0:S].rearrange("p (t d) -> p t d", t=TB), xb_sb[:, bass.ds(b * TB, TB), :], ALU.add).then_inc(res1_done, 1)

            def moments(b):
                wait_from_1(dve, res1_done, b + 1)
                for t in range(TB):
                    last = dve.bn_stats(stats1[:, t, :], res1[:, t, :])
                last.then_inc(bn1_done, 1)
                dve.wait_ge(cast_done, 3)
                dve.wait_ge(bn1_done, b + 1)
                for t in range(TB):
                    last = dve.bn_aggr(mv1[:, t, :], stats1[:, t, :])
                last.then_inc(mv1_done, 1)
                dve.wait_ge(mv1_done, b + 1)
                wait_from_1(dve, rstd1_done, b)
                dve.tensor_scalar(var1[:], mv1[:, :, 1], LN_EPS, None, ALU.add).then_inc(var1_done, 1)

            def layernorm(b):
                wait_from_1(dve, rstd1_done, b + 1)
                for t in range(TB):
                    last = dve.tensor_scalar(x1[:, bass.ds(b * TB + t, 1), :].rearrange("p o d -> p (o d)"), res1[:, t, :], mv1[:, t, 0:1], rstd1[:, t:t + 1], ALU.subtract, ALU.mult)
                last.then_inc(x1_done, 1)

            def batch(b, first, last):
                for k in range(NBANK):
                    if not last:
                        maxima(b + 1, k)
                    if k in (3, 6) and not first:
                        normalise(b - 1, k // 4)
                if not first:
                    residual(b - 1)
                if not last:
                    split_m(b + 1)
                if not first:
                    moments(b - 1)
                    layernorm(b - 1)

            dve.wait_ge(xb_ready, NG)
            for k in range(NBANK):
                maxima(0, k)
            split_m(0)
            batch(0, True, False)
            with dve.Fori(1, B - 1) as b:
                batch(b, False, False)
            batch(B - 1, False, True)
            normalise(B - 1, 0)
            normalise(B - 1, 1)
            residual(B - 1)
            moments(B - 1)
            layernorm(B - 1)

            def low_part(s, q):
                dve.wait_ge(fhi_done, s + 1)
                dve.tensor_tensor(f_lo[q][:], fT_bank, f_hi[q][:].bitcast(F32), ALU.subtract).then_inc(flo_done, 1)

            def over_tiles(row):
                return row.rearrange("p (o e) -> p o e", o=1).broadcast_to((P, GT, E))

            def route(s, rnd, parts):
                done_before = 0

                def done(ins):
                    nonlocal done_before
                    done_before += 1
                    ins.then_inc(rt, 1)

                def ready():
                    dve.wait_ge(rt, ROUTER_STEPS * s + done_before)

                if 0 in parts:
                    dve.wait_ge(gates_done, s + 1)
                    done(dve.tensor_tensor(g_val[:], rout_bank.rearrange("p (t e) -> p t e", t=GT), over_tiles(rout_b[:, rnd, :]), ALU.add))
                    ready()
                    done(dve.tensor_tensor(g_bias[:], g_val[:], over_tiles(rout_gb[:, rnd, :]), ALU.add))
                    ready()
                    other = g_bias[:].rearrange("p t (o e) -> p t o e", o=1).broadcast_to((P, GT, E, E))
                    own = g_bias[:].rearrange("p t (e o) -> p t e o", o=1).broadcast_to((P, GT, E, E))
                    done(dve.tensor_tensor(beats[:], other, own, ALU.is_gt))
                    done(dve.tensor_tensor(ties[:], other, own, ALU.is_equal))
                    ready()
                    flat = ties[:].rearrange("p t e f -> p t (e f)")
                    done(dve.tensor_tensor(flat, flat, before[:].rearrange("p (o n) -> p o n", o=1).broadcast_to((P, GT, E * E)), ALU.mult))
                    assert done_before == ROUTER_FIRST
                if 1 in parts:
                    done_before = ROUTER_FIRST
                    ready()
                    done(dve.tensor_tensor(beats[:], beats[:], ties[:], ALU.add))
                    ready()
                    done(dve.tensor_reduce(rank[:], beats[:], AX.X, ALU.add))
                    ready()
                    done(dve.tensor_scalar(half_sel[:], rank[:], float(TOPK), 0.5, ALU.is_lt, ALU.mult))
                    ready()
                    done(dve.tensor_tensor(sel_g[:], half_sel[:], g_val[:], ALU.mult))
                    ready()
                    done(dve.tensor_reduce(half_sum[:], sel_g[:], AX.X, ALU.add))
                    ready()
                    done(dve.tensor_tensor(g_diff[:], g_val[:], half_sum[:].rearrange("p (t o) -> p t o", o=1).broadcast_to((P, GT, E)), ALU.subtract))
                    assert done_before == ROUTER_STEPS - 3

            def weigh(s):
                dve.wait_ge(tanh_done, s + 1)
                dve.scalar_tensor_tensor(out=w_tok[:], in0=g_tanh[:], scalar=1.0, in1=half_sel[:], op0=ALU.add, op1=ALU.mult).then_inc(rt, 1)
                dve.wait_ge(rt, ROUTER_STEPS * s + ROUTER_STEPS - 2)
                dve.tensor_copy(w_tok_s[:, :, 0:E], w_tok[:]).then_inc(rt, 1)
                dve.wait_ge(rt, ROUTER_STEPS * s + ROUTER_STEPS - 1)
                dve.tensor_tensor(w_tok_s[:, :, E:2 * E], w_tok[:], w_tok_s[:, :, 0:E].bitcast(F32), ALU.subtract).then_inc(rt, 1)

            def unit(s, u):
                e = weights_of(u)
                up_b = b_cols[:, e:e + 1] if e < E else b_cols[:, E + e:E + e + 1]
                if u < NS:
                    wait_from_1(dve, silu_done, N * s + u + 1)
                    dst, factor = hid_s[u], silu[u]
                else:
                    wait_from_1(dve, silu_w_done, E * s + e + 1)
                    if e >= 2:
                        wait_from_1(dve, down_done, (E + 1) * s + e)
                    dst, factor = hid_w[e % 2], silu_w[e % 2]
                dve.wait_ge(up_done, N * s + u + 1)
                dve.scalar_tensor_tensor(out=dst[:], in0=up_bank, scalar=up_b, in1=factor[:], op0=ALU.add, op1=ALU.mult).then_inc(hid_done, 1)

            def add_residual(s, g, q, rnd):
                wait_from_1(dve, down_done, (E + 1) * (s + 1))
                src = x1[:, bass.ds(g * GT, GT), :] if rnd == 0 else y_out[q][:]
                dve.tensor_tensor(y_sum[q][:], down_bank[q].rearrange("p (t d) -> p t d", t=GT), src, ALU.add).then_inc(ysum_done, 1)

            def mean_square(s):
                dve.wait_ge(ssq_done, s + 1)
                dve.tensor_scalar(ms[:], ssq[:], 1.0 / D, FF_EPS, ALU.mult, ALU.add).then_inc(ms_done, 1)

            def rms_norm(s, q, rnd):
                dve.wait_ge(rms_done, s + 1)
                dst = y_out[q] if rnd == 0 else y_end[q]
                for t in range(GT):
                    last = dve.scalar_tensor_tensor(out=dst[:, t, :], in0=y_sum[q][:, t, :], scalar=rms_inv[:, t:t + 1], in1=norm_all[:, rnd, :], op0=ALU.mult, op1=ALU.mult)
                last.then_inc(y_done, 1)

            def end_residual(s, g, q):
                dve.wait_ge(y_done, s + 1)
                dve.tensor_tensor(x_end[q][:], x1[:, bass.ds(g * GT, GT), :], y_end[q][:], ALU.add).then_inc(xend_done, 1)

            def end_moments(g, q):
                wait_from_1(dve, xend_done, g + 1)
                for t in range(GT):
                    last = dve.bn_stats(stats2[:, t, :], x_end[q][:, t, :])
                last.then_inc(bn2_done, 1)
                dve.wait_ge(cast_done, 3)
                wait_from_1(dve, bn2_done, g + 1)
                for t in range(GT):
                    last = dve.bn_aggr(mv2[:, t, :], stats2[:, t, :])
                last.then_inc(mv2_done, 1)
                dve.wait_ge(mv2_done, g + 1)
                dve.tensor_scalar(var2[:], mv2[:, :, 1], LN_EPS, None, ALU.add).then_inc(var2_done, 1)

            def end_norm(g, q):
                dve.wait_ge(rstd2_done, g + 1)
                for t in range(GT):
                    last = dve.tensor_scalar(xb_sb[:, bass.ds(g * GT + t, 1), :].rearrange("p o d -> p (o d)"), x_end[q][:, t, :], mv2[:, t, 0:1], rstd2[:, t:t + 1], ALU.subtract, ALU.mult)
                last.then_inc(o_ready, 1)

            low_part(0, 0)
            route(0, 0, range(2))
            with dve.Fori(0, NG // 2) as pair:
                steps = steps_of(pair)

                def behind(n, u):
                    s, q, rnd = steps[n]
                    g = 2 * pair + q
                    if u == 0:
                        add_residual(s, g, q, rnd)
                    if u == 2:
                        mean_square(s)
                    if u == 3:
                        rms_norm(s, q, rnd)
                    if rnd == C - 1:
                        if u == 4:
                            end_residual(s, g, q)
                        if u == 5:
                            end_moments(g, q)
                        if u == 6:
                            end_norm(g, q)

                for n, (s, q, rnd) in enumerate(steps):
                    next_rnd = rnd if q == 0 else 1 - rnd
                    for u in range(N):
                        unit(s, u)
                        if u == 0:
                            weigh(s)
                        if u == 4:
                            low_part(s + 1, 1 - q)
                        if n:
                            behind(n - 1, u)
                        if u in (6, 7):
                            route(s + 1, next_rnd, (u - 6,))
                for u in range(N):
                    behind(3, u)

        @block.tensor
        def _(pe):
            start_from_1(pe, "pe")
            pe.wait_ge(c_loaded, 16 * 5)
            pe.wait_ge(ones_ready, 3)
            pe.wait_ge(bq_cols, 1)
            pe.matmul(banks[:, 7, 0:1], bq_perm[:], scale_one[:]).then_inc(bq_made, 1)
            pe.wait_ge(bq_ready, 1)
            pe.wait_ge(w_split, 6)
            PASSES = ((w_hi, xT_hi), (w_hi, xT_lo), (w_lo, xT_hi))

            def transpose_x(g):
                pe.wait_ge(x_loaded[g], 16)
                wait(pe, xlo_done, g - 1)
                for t in range(GT):
                    last = pe.transpose(banks[:, g % 2, P * t:P * t + P], x_sb[:, GT * g + t, :], ident[:])
                last.then_inc(xT_done, 1)

            transpose_x(0)
            for g in range(NG):
                if g + 1 < NG:
                    transpose_x(g + 1)
                pe.wait_ge(xhi_done, g + 1)
                pe.wait_ge(xlo_done, g + 1)
                for n in range(2):
                    wait(pe, qkl_done, 2 * (g - 1) + n + 1)
                    for k, (w, xt) in enumerate(PASSES):
                        last = pe.matmul(banks[:, 2 + n, :], w[:, n, :], xt[:, g % 2, :], start=(k == 0), stop=(k == 2))
                    last.then_inc(qkv_done, 1)
                wait(pe, v_copied, g)
                for t in range(GT):
                    for k, (w, xt) in enumerate(PASSES):
                        last = pe.matmul(banks[:, 4, P * t:P * t + P], xt[:, g % 2, P * t:P * t + P], w[:, 2, :], start=(k == 0), stop=(k == 2))
                last.then_inc(qkv_done, 1)

            def scores_for_max(b, p, nth, k):
                u, part = divmod(k, 3)
                if part == 0:
                    pe.wait_ge(st_in[p][u], 32 * nth)
                wait(pe, max_done, NBANK * b + k - 1)
                bank = max_bank[k % 2]
                if part == 0:
                    heads, width, keys, q0 = HU, P, P, 0
                else:
                    heads, width, keys, q0 = 2, S, S, P
                pe.matmul(bank.rearrange("p (h k) -> p h k", h=heads)[:, :, width - P:width], ident_bf[:], causal_bf[:, 0:heads, :],
                          start=True, stop=False, skip_group_check=True)
                for j in range(heads):
                    h = HU * u + 2 * max(part - 1, 0) + j
                    last = pe.matmul(bank[:, width * j:width * (j + 1)], q_st[p][0:ROWS_MAX, h, q0:q0 + P], k_st[p][0:ROWS_MAX, h, 0:keys],
                                     start=False, stop=True, skip_group_check=True)
                last.then_inc(s_done, 1)

            def scores_for_exp(b, p, nth, u):
                n = 4 * b + u
                pe.wait_ge(m_in[p][u], 16 * nth)
                wait(pe, exp_done, 2 * n - 1)
                for j in range(HU):
                    h = HU * u + j
                    last = pe.matmul(exp_bank0[:, S * j:S * j + S], k_st[p][0:ROWS_EXP, h, 0:P], q_st[p][0:ROWS_EXP, h, :])
                last.then_inc(st_done, 1)
                wait(pe, exp_done, 2 * n)
                for j in range(HU):
                    h = HU * u + j
                    last = pe.matmul(exp_bank1[:, P * j:P * j + P], k_st[p][0:ROWS_EXP, h, P:S], q_st[p][0:ROWS_EXP, h, P:S])
                last.then_inc(st_done, 1)

            def product_with_v(b, p, u):
                n = 4 * b + u
                r = u % 2
                if u == 0:
                    pe.wait_ge(v_ready, b + 1)
                wait(pe, ot_copied, n - 1)
                pe.wait_ge(sel_done, 2 * n + 1)
                for j in range(HU):
                    pe.matmul(av_bank[r][32 * j:32 * j + 32, :], v_st[p][:, 0, HU * u + j, :], probs[r][:, S * j:S * j + S],
                              start=True, stop=False, skip_group_check=True, tile_position=(0, 32 * j))
                pe.wait_ge(sel_done, 2 * n + 2)
                for j in range(HU):
                    last = pe.matmul(av_bank[r][32 * j:32 * j + 32, P:S], v_st[p][:, 1, HU * u + j, :], probs[r][:, HU * S + P * j:HU * S + P * j + P],
                                     start=False, stop=True, skip_group_check=True, tile_position=(0, 32 * j))
                last.then_inc(av_done, 1)

            def transpose_m(b):
                pe.wait_ge(m_lo, b + 1)
                wait_from_1(pe, res1_done, b - 1)
                for t in range(TB):
                    last = pe.transpose(misc[0:2 * H, P * t:P * t + P], m_split[:, t, :].bitcast(F32), ident[:])
                last.then_inc(mT_done, 1)

            def transpose_o(b, p, t):
                if t == 0:
                    pe.wait_ge(ot_copied, 4 * (b + 1))
                    pe.wait_ge(mT_copied, min(b + 2, B) if isinstance(b, int) else b + 2)
                    wait_from_1(pe, res1_done, b)
                else:
                    wait_from_1(pe, norm_done, 2 * b + 1)
                for u in range(U):
                    last = pe.transpose(misc[:, P * u:P * u + P], o_t[p][:, u, P * t:P * t + P], ident[:])
                last.then_inc(oT_done, 1)

            def transpose_norm(b):
                wait_from_1(pe, norm_done, 2 * b + 2)
                for t in range(TB):
                    last = pe.transpose(misc[:, P * t:P * t + P], o_norm[:, t, :], ident[:])
                last.then_inc(onT_done, 1)

            def project(b):
                pe.wait_ge(onT_copied, b + 1)
                for t in range(TB):
                    last = pe.matmul(misc[:, P * t:P * t + P], o_norm_t[:, P * t:P * t + P], wo[:])
                last.then_inc(proj_done, 1)

            def batch(b, p, nth, first, last):
                def maxima(*ks):
                    if not last:
                        for k in ks:
                            scores_for_max(b + 1, 1 - p, nth + p, k)

                maxima(0, 1)
                scores_for_exp(b, p, nth, 0)
                maxima(2)
                if not first:
                    transpose_o(b - 1, 1 - p, 0)
                maxima(3, 4)
                scores_for_exp(b, p, nth, 1)
                maxima(5)
                if not first:
                    transpose_o(b - 1, 1 - p, 1)
                product_with_v(b, p, 0)
                maxima(6, 7)
                scores_for_exp(b, p, nth, 2)
                if not first:
                    transpose_norm(b - 1)
                maxima(8, 9)
                product_with_v(b, p, 1)
                maxima(10)
                if not first:
                    project(b - 1)
                maxima(11)
                scores_for_exp(b, p, nth, 3)
                product_with_v(b, p, 2)
                if not last:
                    transpose_m(b + 1)
                product_with_v(b, p, 3)

            pe.wait_ge(fw_in, 16 * 19)
            for half in range(2):
                for n in range(4):
                    last = pe.transpose(banks[:, 5 + half, P * n:P * n + P], up_w[:, 4 * half + n, :], ident[:])
                last.then_inc(upT_done, 1)
            pe.transpose(banks[:, 7, 0:2 * E + NS + 1], b_rows[:], ident[0:2 * E + NS + 1, 0:2 * E + NS + 1]).then_inc(bcol_done, 1)
            for half in range(2):
                pe.wait_ge(upT_copied, half + 1)
                for n in range(4):
                    e = 4 * half + n
                    last = pe.matmul(banks[:, 5 + half, P * n:P * n + P], up_t[:, e, :], gate_w[:, min(e, E), :])
                last.then_inc(wg_made, 1)
            pe.wait_ge(bcol_copied, 1)
            for e in range(N):
                col = e if e < E else E + e
                last = pe.matmul(banks[:, 7, e:e + 1], gate_w[:, min(e, E), :], b_cols[:, col:col + 1])
            last.then_inc(bg_made, 1)
            pe.wait_ge(fw_lo, 3)
            pe.wait_ge(gb_ready, 2)
            pe.wait_ge(rw_split, 3)
            pe.wait_ge(const_in, 16 * 6)
            pe.wait_ge(xlo_done, NG)
            pe.wait_ge(qkl_done, 2 * NG)
            pe.wait_ge(v_copied, NG)
            for k in range(NBANK):
                scores_for_max(0, 0, 1, k)
            transpose_m(0)
            batch(0, 0, 1, True, False)
            with pe.Fori(0, B // 2 - 1) as pair:
                batch(2 * pair + 1, 1, pair + 1, False, False)
                batch(2 * pair + 2, 0, pair + 2, False, False)
            batch(B - 1, 1, B // 2, False, True)
            transpose_o(B - 1, 1, 0)
            transpose_o(B - 1, 1, 1)
            transpose_norm(B - 1)
            project(B - 1)

            def three_passes(bank, w_h, w_l, q, done):
                for k, (w, f) in enumerate(((w_h, f_hi), (w_h, f_lo), (w_l, f_hi))):
                    last = pe.matmul(bank, w, f[q][:], start=(k == 0), stop=(k == 2))
                last.then_inc(done, 1)

            def transposes(s, q, src, produced, count):
                pe.wait_ge(produced, count)
                wait_from_1(pe, flo_done, s)
                for t in range(GT):
                    last = pe.transpose(fT_bank[:, P * t:P * t + P], src[:, t, :], ident[:])
                last.then_inc(fT_done, 1)

            def gates(s, q, rnd):
                pe.wait_ge(fhi_done, s + 1)
                wait_from_1(pe, flo_done, s + 1)
                for t in range(GT):
                    for k, (f, w) in enumerate(((f_hi, rout_hi), (f_hi, rout_lo), (f_lo, rout_hi))):
                        last = pe.matmul(rout_bank[:, E * t:E * t + E], f[q][:, P * t:P * t + P], w[:, rnd, :], start=(k == 0), stop=(k == 2))
                last.then_inc(gates_done, 1)

            def weights_t(s):
                pe.wait_ge(rt, ROUTER_STEPS * (s + 1))
                wait_from_1(pe, wT_copied, s)
                for t in range(GT):
                    last = pe.transpose(wT_bank[:, P * t:P * t + P], w_tok_s[:, t, :].bitcast(F32), ident[:])
                last.then_inc(wT_done, 1)

            def down(s, q, tile, w, first, last_one):
                for t in range(GT):
                    last = pe.matmul(down_bank[q][:, P * t:P * t + P], tile[:, P * t:P * t + P], w, start=(first and t == 0), stop=last_one, skip_group_check=True)
                return last

            wait_from_1(pe, res1_done, B)
            pe.wait_ge(exp_done, 8 * B)
            pe.wait_ge(ot_copied, 4 * B)
            transposes(0, 0, x_in[0], xin_ready, 1)
            gates(0, 0, 0)
            def gate(s, q, u):
                wait_from_1(pe, silu_done, N * s + u)
                three_passes(gate_bank, gate_hi[:, weights_of(u), :], gate_lo[:, weights_of(u), :], q, gate_done)

            gate(0, 0, 0)
            with pe.Fori(0, NG // 2) as pair:
                def up(s, q, u):
                    wait_from_1(pe, hid_done, N * s + u)
                    three_passes(up_bank, up_hi[:, weights_of(u), :], up_lo[:, weights_of(u), :], q, up_done)

                def expert_weights(s, q, e):
                    wait_from_1(pe, wb_copied, E * s + e)
                    pe.matmul(wb_bank, unit_rows_r[:, e, :], w_t[q][0:2 * E, :]).then_inc(wb_done, 1)

                def down_expert(s, q, e):
                    wait_from_1(pe, hid_done, N * s + NS + e + 1)
                    down(s, q, hid_w[e % 2], down_w[:, e, :], False, e == E - 1).then_inc(down_done, 1)

                for n, (s, q, rnd) in enumerate(steps_of(pair)):
                    for u in range(N):
                        if NS < u + 1 < N:
                            expert_weights(s, q, u + 1 - NS)
                        if u + 1 < N:
                            gate(s, q, u + 1)
                        if u == 1:
                            weights_t(s)
                        up(s, q, u)
                        if u == N - 1:
                            gate(s + 1, 1 - q, 0)
                        if u == 0:
                            if n:
                                down_expert(s - 1, 1 - q, E - 1)
                        elif u == 1:
                            wait_from_1(pe, wT_copied, s + 1)
                            expert_weights(s, q, 0)
                            wait_from_1(pe, ysum_done, s if n == 0 else s - 1)
                            down(s, q, w_t[q].bitcast(F32), down_b[:], True, False)
                        elif u == 2:
                            pe.wait_ge(hsum_done, s + 1)
                            down(s, q, hid_sum, down_w[:, E, :], False, False).then_inc(down_done, 1)
                        else:
                            down_expert(s, q, u - 3)
                        if u == 4:
                            if n == 0:
                                transposes(s + 1, 1, x_in[1], xin_ready, 2 * pair + 2)
                            elif n == 3:
                                transposes(s + 1, 0, x_in[0], xin_ready, 2 * pair + 3)
                            else:
                                transposes(s + 1, 1 - q, y_out[1 - q], y_done, s)
                        if u == 5:
                            gates(s + 1, 1 - q, rnd if q == 0 else 1 - rnd)
                down_expert(4 * pair + 3, 1, E - 1)


_INS = ['L0_attn_x', 'L0_attn_Wq', 'L0_attn_bq', 'L0_attn_Wk', 'L0_attn_Wv', 'L0_attn_Wo', 'L0_attn_bo',
        'L0_ffn_router_W', 'L0_ffn_router_b', 'L0_ffn_gate_bias', 'L0_ffn_exp_Wup', 'L0_ffn_exp_bup', 'L0_ffn_exp_Wg', 'L0_ffn_exp_bg',
        'L0_ffn_exp_Wdown', 'L0_ffn_exp_bdown', 'L0_ffn_share_Wup', 'L0_ffn_share_bup', 'L0_ffn_share_Wg', 'L0_ffn_share_bg',
        'L0_ffn_share_Wdown', 'L0_ffn_share_bdown', 'L0_ffn_norm_w']


def constants():
    import numpy as np
    ident = np.eye(P, dtype=np.float32)
    causal = np.where(np.arange(P)[None, :] > np.arange(P)[:, None], np.float32(-1e30), np.float32(0)).astype(np.float32)
    slopes = (2.0 ** (-8.0 * np.arange(1, H + 1, dtype=np.float32) / H)).astype(np.float32)
    alibi = -(slopes[:, None] * np.arange(S, dtype=np.float32)[None, :]).astype(np.float32)
    hi = (alibi.view(np.uint32) & np.uint32(0xFFFFF000)).view(np.float32)
    of_head = np.zeros((2, H, H, S), np.float32)
    for h in range(H):
        of_head[:, h, h, :] = 1
    rows = np.concatenate([hi[None], (alibi - hi)[None], np.ones((2, H, S), np.float32), of_head.reshape(2 * H, H, S)])
    unit = np.zeros((2, E, E, P), np.float32)
    for e in range(E):
        unit[:, e, e, :] = 1
    before = np.zeros((P, E, E), np.float32)
    before[:] = np.arange(E)[None, :] < np.arange(E)[:, None]
    return {"ident_c": ident, "causal_c": causal, "alibi_c": rows, "unit_c": unit.reshape(2 * E, E * P),
            "before_c": before.reshape(P, E * E)}


def kernel(**inputs):
    import numpy as _np
    import concourse.bacc as _bacc
    from concourse import mybir as _mybir
    from concourse.bass_utils import run_bass_kernel_spmd as _run

    nc = _bacc.Bacc("TRN2", target_bir_lowering=False, num_devices=1)
    arrays, args = {}, []
    for name, a in [(n, inputs[n]) for n in _INS] + list(constants().items()):
        a = _np.ascontiguousarray(a)
        arrays[f"in_{name}_dram"] = a
        args.append(nc.dram_tensor(f"in_{name}_dram", a.shape, _mybir.dt.from_np(a.dtype), kind="ExternalInput").ap())
    args.append(nc.dram_tensor("out_0_dram", (B, S, D), F32, kind="ExternalOutput").ap())
    program(nc, *args)
    r = _run(nc, [arrays], core_ids=[0])
    return r.results[0]["out_0_dram"]
```

```python
from contextlib import ExitStack

import concourse.bass as bass
from concourse import mybir

F32 = mybir.dt.float32
F32R = mybir.dt.float32r
BF16 = mybir.dt.bfloat16
ALU = mybir.AluOpType
ACT = mybir.ActivationFunctionType
AX = mybir.AxisListType

P = 128
B, S, D = 8, 256, 128
H, HD = 16, 8
TB = S // P
NT = B * TB
GT = 4
NG = NT // GT
GW = GT * P
U = 4
HU = H // U
NBANK = 3 * U
ROWS_MAX = 96
ROWS_EXP = 128
FW_FIRST, FW_REST = 8, 14
QSCALE = float(HD) ** -0.5
WARM_FIRST, WARM_SPLITS, WARM_END = 7, 3, 2
LN_EPS = 1e-5
C, E, TOPK = 2, 6, 2
NS = 2
BIAS_ROWS = 3 * E + NS
N = E + NS
FF_EPS = 1e-6
ROUTER_STEPS = 16
ROUTER_FIRST = 6


def program(nc, x, Wq, bq, Wk, Wv, Wo, bo, router_W, router_b, gate_bias, exp_Wup, exp_bup, exp_Wg, exp_bg,
            exp_Wdown, exp_bdown, share_Wup, share_bup, share_Wg, share_bg, share_Wdown, share_bdown, norm_w,
            ident_c, causal_c, alibi_c, unit_c, before_c, signs_c, out):
    ctx = ExitStack()
    with ctx:
        def sb(name, shape, dt=F32):
            return ctx.enter_context(nc.sbuf_tensor(name, shape, dt))

        def sem(name):
            return ctx.enter_context(nc.semaphore(name))

        banks = ctx.enter_context(nc.psum_tensor("banks", [P, 8, 512], F32))

        ident = sb("ident", [P, P])
        ident_bf = sb("ident_bf", [P, P], BF16)
        causal = sb("causal", [P, P])
        step = sb("step", [1, 2])
        causal_bf = sb("causal_bf", [P, 4, P], BF16)
        w_in = sb("w_in", [P, 3, P])
        wqs = sb("wqs", [P, P])
        w_hi = sb("w_hi", [P, 3, P], F32R)
        w_lo = sb("w_lo", [P, 3, P], F32R)
        wo = sb("wo", [P, P])
        bo_all = sb("bo_all", [P, P])
        bq_row = sb("bq_row", [1, P])
        bq_perm = sb("bq_perm", [1, P])
        scale_one = sb("scale_one", [1, 1])
        bq_col = sb("bq_col", [P, 1])
        minus_half = sb("minus_half", [P, GT])

        x_sb = sb("x_sb", [P, NT, D])
        xb_sb = sb("xb_sb", [P, NT, D])
        v_sb = sb("v_sb", [P, NT, D])
        x1 = sb("x1", [P, NT, D])
        xT_hi = sb("xT_hi", [P, 2, GW], F32R)
        xT_lo = sb("xT_lo", [P, 2, GW], F32R)
        qk_parts = [sb(f"qk_parts{g}", [P, 4, GW], F32R)[:] for g in range(2)]

        up_w = sb("up_w", [P, N, P])
        gate_w = sb("gate_w", [P, E + 1, P])
        up_t = sb("up_t", [P, N, P])
        down_w = sb("down_w", [P, E + 1, P])
        up_gate = sb("up_gate", [P, 4, N, P], F32R)
        up_hi, up_lo, gate_hi, gate_lo = (up_gate[:, n] for n in range(4))
        down_b = sb("down_b", [BIAS_ROWS, P])
        down_b_hi = sb("down_b_hi", [BIAS_ROWS, P], F32R)
        down_b_lo = sb("down_b_lo", [BIAS_ROWS, P])
        down_b_parts = sb("down_b_parts", [BIAS_ROWS, P], F32R)
        part_signs = sb("part_signs", [BIAS_ROWS, 2])
        b_rows = sb("b_rows", [2 * E + NS + 1, P])
        b_cols = sb("b_cols", [P, 2 * E + NS + 1])
        gate_b = sb("gate_b", [P, N])
        unit_rows = sb("unit_rows", [2 * E, E * P])
        unit_rows_r = sb("unit_rows_r", [2 * E, E, P], F32R)
        before = sb("before", [P, E * E])
        rout_w = sb("rout_w", [P, C, E])
        rout_parts = sb("rout_parts", [P, C, 2 * E], F32R)
        rout_b = sb("rout_b", [P, C, E])
        rout_gb = sb("rout_gb", [P, C, E])
        norm_all = sb("norm_all", [P, C, D])

        attention = ExitStack()

        def sba(name, shape, dt=F32):
            return attention.enter_context(nc.sbuf_tensor(name, shape, dt))

        q_st, k_st = [], []
        for p in range(2):
            q_st.append(sba(f"q_st{p}", [P, H, S], F32R))
            k_st.append(sba(f"k_st{p}", [P, H, S], F32R))
        v_st = [sba(f"v_st{p}", [P, TB, H, 32]) for p in range(2)]
        m_neg = sba("m_neg", [P, TB, H])
        m_split = sba("m_split", [P, TB, 2 * H], F32R)
        m_rows = sba("m_rows", [2 * H, S], F32R)
        probs = [sba(f"probs{r}", [P, HU * S + HU * P]) for r in range(2)]
        o_t = [sba(f"o_t{p}", [P, U, S]) for p in range(2)]
        den_inv = sba("den_inv", [P, H])
        o_norm = sba("o_norm", [P, TB, D])
        o_norm_t = sba("o_norm_t", [P, S])
        res1 = sba("res1", [P, TB, D])
        stats1 = sba("stats1", [P, TB, 6])
        mv1 = sba("mv1", [P, TB, 2])
        var1 = sba("var1", [P, TB])
        rstd1 = sba("rstd1", [P, TB])

        attention.close()
        x_in = [sb(f"x_in{q}", [P, GT, D]) for q in range(2)]
        f_hi = [sb(f"f_hi{q}", [P, GW], F32R) for q in range(2)]
        f_lo = [sb(f"f_lo{q}", [P, GW], F32R) for q in range(2)]
        g_part = sb("g_part", [P, GT, E])
        g_val = sb("g_val", [P, GT, E])
        g_bias = sb("g_bias", [P, GT, E])
        beats = sb("beats", [P, GT, E, E])
        ties = sb("ties", [P, GT, E, E])
        rank = sb("rank", [P, GT, E])
        half_sel = sb("half_sel", [P, GT, E])
        sel_g = sb("sel_g", [P, GT, E])
        half_sum = sb("half_sum", [P, GT])
        g_diff = sb("g_diff", [P, GT, E])
        g_tanh = sb("g_tanh", [P, GT, E])
        w_tok = sb("w_tok", [P, GT, E])
        w_tok_s = sb("w_tok_s", [P, GT, 3 * E], F32R)
        w_t = [sb(f"w_t{q}", [BIAS_ROWS, GW], F32R) for q in range(2)]
        silu = [sb(f"silu{r}", [P, GW]) for r in range(2)]
        hid_s = [sb(f"hid_s{r}", [P, GW]) for r in range(2)]
        y_out = [sb(f"y_out{q}", [P, GT, D]) for q in range(2)]
        y_sum = [sb(f"y_sum{q}", [P, GT, D]) for q in range(2)]
        y_end = [sb(f"y_end{q}", [P, GT, D]) for q in range(2)]
        x_end = [sb(f"x_end{q}", [P, GT, D]) for q in range(2)]
        wb_sb = [sb(f"wb_sb{r}", [P, GW]) for r in range(2)]
        silu_w = [sb(f"silu_w{r}", [P, GW]) for r in range(2)]
        hid_w = [sb(f"hid_w{r}", [P, GW]) for r in range(2)]
        hid_sum = sb("hid_sum", [P, GW])
        squares = sb("squares", [P, GT, D])
        ms = sb("ms", [P, GT])
        rms_inv = sb("rms_inv", [P, GT])
        stats2 = sb("stats2", [P, GT, 6])
        mv2 = sb("mv2", [P, GT, 2])
        var2 = sb("var2", [P, GT])
        rstd2 = sb("rstd2", [P, GT])

        for later in (xb_sb, x1):
            qk_parts.append(later[:].rearrange("p (n t) d -> p n (t d)", n=4).bitcast(F32R))

        qk_rows = nc.dram_tensor("qk_rows", [4, HD * H, B * S], F32, kind="Internal").ap()
        const_rows = nc.dram_tensor("const_rows", [4 + 2 * H, H, S], F32, kind="Internal").ap()

        x_loaded = [sem(f"x_loaded{g}") for g in range(NG)]
        w_loaded = sem("w_loaded")
        ident_loaded = sem("ident_loaded")
        bq_loaded = sem("bq_loaded")
        causal_loaded = sem("causal_loaded")
        o_loaded = sem("o_loaded")
        warm_zero = sem("warm_zero")
        wq_scaled = sem("wq_scaled")
        cast_done = sem("cast_done")
        w_split = sem("w_split")
        bq_cols = sem("bq_cols")
        bq_made = sem("bq_made")
        bq_ready = sem("bq_ready")
        ones_ready = sem("ones_ready")
        xb_ready = sem("xb_ready")
        st_zero = sem("st_zero")
        const_copied = sem("const_copied")
        const_in = [sem(f"const_in{p}") for p in range(2)]
        xT_done = sem("xT_done")
        xhi_done = sem("xhi_done")
        xlo_done = sem("xlo_done")
        qkv_done = sem("qkv_done")
        qkh_done = sem("qkh_done")
        qkl_done = sem("qkl_done")
        v_copied = sem("v_copied")
        rows_out = [sem(f"rows_out{g}") for g in range(NG)]
        st_in = [[sem(f"st_in{p}{half}") for half in range(2)] for p in range(2)]
        s_done = sem("s_done")
        max_done = sem("max_done")
        m_hi = sem("m_hi")
        m_lo = sem("m_lo")
        mT_done = sem("mT_done")
        mT_copied = sem("mT_copied")
        m_in = [[sem(f"m_in{p}{u}") for u in range(U)] for p in range(2)]
        st_done = sem("st_done")
        exp_done = sem("exp_done")
        sel_done = sem("sel_done")
        step_done = sem("step_done")
        v_ready = sem("v_ready")
        v_const = sem("v_const")
        av_done = sem("av_done")
        ot_copied = sem("ot_copied")
        oT_done = sem("oT_done")
        den_done = sem("den_done")
        norm_done = sem("norm_done")
        onT_done = sem("onT_done")
        onT_copied = sem("onT_copied")
        proj_done = sem("proj_done")
        res1_done = sem("res1_done")
        bn1_done = sem("bn1_done")
        mv1_done = sem("mv1_done")
        var1_done = sem("var1_done")
        rstd1_done = sem("rstd1_done")
        x1_done = sem("x1_done")
        out_done = sem("out_done")
        fw_first = sem("fw_first")
        fw_in = sem("fw_in")
        upT_done = sem("upT_done")
        upT_copied = sem("upT_copied")
        wg_made = sem("wg_made")
        fw_hi = sem("fw_hi")
        fw_lo = sem("fw_lo")
        bcol_done = sem("bcol_done")
        bcol_copied = sem("bcol_copied")
        bg_made = sem("bg_made")
        gb_ready = sem("gb_ready")
        rw_split = sem("rw_split")
        wt_ready = sem("wt_ready")
        xin_ready = sem("xin_ready")
        fT_done = sem("fT_done")
        fhi_done = sem("fhi_done")
        flo_done = sem("flo_done")
        gates_done = sem("gates_done")
        router_done = sem("router_done")
        tanh_done = sem("tanh_done")
        wT_done = sem("wT_done")
        wT_copied = sem("wT_copied")
        gate_done = sem("gate_done")
        up_done = sem("up_done")
        wb_done = sem("wb_done")
        silu_done = sem("silu_done")
        hid_done = sem("hid_done")
        wb_copied = sem("wb_copied")
        silu_w_done = sem("silu_w_done")
        hsum_done = sem("hsum_done")
        down_done = sem("down_done")
        ysum_done = sem("ysum_done")
        ms_done = sem("ms_done")
        rms_done = sem("rms_done")
        y_done = sem("y_done")
        xend_done = sem("xend_done")
        centred = sem("centred")
        bn2_done = sem("bn2_done")
        mv2_done = sem("mv2_done")
        var2_done = sem("var2_done")
        rstd2_done = sem("rstd2_done")
        o_ready = sem("o_ready")

        def wait(eng, s, value):
            if not isinstance(value, int) or value > 0:
                eng.wait_ge(s, value)

        from_1 = {"pe": (oT_done, onT_done, proj_done, av_done, down_done),
                  "dve": (res1_done, norm_done, x1_done, hid_done, ms_done, xend_done, bn2_done, var2_done, ysum_done, flo_done),
                  "act": (silu_done, wT_copied, wb_copied),
                  "pool": (rstd1_done, silu_w_done)}

        def wait_from_1(eng, s, value):
            if not isinstance(value, int) or value > 0:
                eng.wait_ge(s, value + 1)

        def start_from_1(eng, name):
            for s in from_1[name]:
                eng.sem_inc(s, 1)

        max_bank = [banks[:, 0, :], banks[:, 1, :]]
        exp_bank0 = banks[:, 2:4, :].rearrange("p a c -> p (a c)")
        exp_bank1 = banks[:, 4, :]
        av_bank = [banks[:, 5, 0:S], banks[:, 6, 0:S]]
        mT_bank = banks[0:2 * H, 6, S:2 * S]
        misc = banks[:, 7, :]

        fT_bank, rout_bank = banks[:, 0, :], banks[:, 1, 0:GT * 2 * E]
        wT_bank = banks[0:3 * E, 0, :]
        gate_bank, wb_bank = banks[:, 2, :], banks[:, 4, :]
        up_bank = [banks[:, 3, :], banks[:, 5, :]]
        down_bank = [banks[:, 6, :], banks[:, 7, :]]

        def qkv_banks(g):
            return (2, 3, 4) if g % 2 == 0 else (5, 6, 7)

        steps = [(2 * pair + q, rnd) for pair in range(NG // 2) for rnd in range(C) for q in range(2)]

        def weights_of(u):
            return E + u if u < NS else u - NS

        block = ctx.enter_context(nc.Block())

        @block.sync
        def _(sp):
            x_tiles = x.rearrange("b (u p) d -> p (b u) d", p=P)
            def load_x(g):
                sp.dma_start(x_sb[:, GT * g:GT * g + GT, :], x_tiles[:, GT * g:GT * g + GT, :]).then_inc(x_loaded[g], 16)

            load_x(0)
            for n, w in ((1, Wk), (2, Wv)):
                sp.dma_start(w_in[:, n, :], w).then_inc(w_loaded, 16)
            load_x(1)
            sp.dma_start(const_rows, alibi_c).then_inc(const_copied, 16)
            load_x(2)
            load_x(3)
            sp.dma_start(bo_all[:], bo.rearrange("(o d) -> o d", o=1).broadcast_to((P, D))).then_inc(o_loaded, 16)
            sp.dma_start(wo[:], Wo).then_inc(o_loaded, 16)

            sp.dma_start(up_w[:, 0:E, :], exp_Wup.rearrange("e h i -> h e i")).then_inc(fw_first, 16)
            sp.dma_start(up_w[:, E:N, :], share_Wup.rearrange("h (s i) -> h s i", s=NS)).then_inc(fw_first, 16)
            sp.dma_start(gate_w[:, 0:E, :], exp_Wg.rearrange("e h i -> h e i")).then_inc(fw_first, 16)
            sp.dma_start(gate_w[:, E, :], share_Wg).then_inc(fw_first, 16)
            sp.dma_start(b_rows[0:E, :], exp_bup).then_inc(fw_first, 16)
            sp.dma_start(b_rows[E:2 * E, :], exp_bg).then_inc(fw_first, 16)
            sp.dma_start(b_rows[2 * E:2 * E + NS, :], share_bup.rearrange("(s d) -> s d", s=NS)).then_inc(fw_first, 16)
            sp.dma_start(b_rows[2 * E + NS:2 * E + NS + 1, :], share_bg.rearrange("(o d) -> o d", o=1)).then_inc(fw_first, 16)

            def const_rows_in(p):
                sp.wait_ge(st_zero, 2 * p + 2)
                sp.dma_start(k_st[p][24:26, :, :].bitcast(F32), const_rows[0:2]).then_inc(const_in[p], 16)
                sp.dma_start(q_st[p][24:26, :, :].bitcast(F32), const_rows[2:4]).then_inc(const_in[p], 16)
                sp.dma_start(k_st[p][ROWS_MAX:ROWS_EXP, :, :].bitcast(F32), const_rows[4:4 + 2 * H]).then_inc(const_in[p], 16)

            def rows_to_dram(g):
                sp.wait_ge(qkh_done, 2 * g + 2)
                sp.wait_ge(qkl_done, 2 * g + 2)
                sp.dma_start(qk_rows[:, :, g * GW:(g + 1) * GW].rearrange("n r t -> r n t"), qk_parts[g].bitcast(F32)).then_inc(rows_out[g], 16)

            def stacks_in(b, p, half):
                heads = slice(H // 2 * half, H // 2 * (half + 1))
                for dst, row, n, parts in ((q_st, 0, 0, 1), (q_st, HD, 0, 2), (k_st, 0, 2, 2), (k_st, 2 * HD, 3, 1)):
                    sp.dma_start(dst[p][row:row + parts * HD, heads, :].bitcast(F32),
                                 qk_rows[n:n + parts, :, bass.ds(b * S, S)].rearrange("n (d h) t -> (n d) h t", h=H)[:, heads, :]
                                 ).then_inc(st_in[p][half], 16)

            def m_rows_in(b, p):
                sp.wait_ge(mT_copied, b + 1)
                for u in range(U):
                    sp.dma_start(q_st[p][ROWS_MAX:ROWS_EXP, HU * u:HU * (u + 1), :].bitcast(F32),
                                 m_rows[:].bitcast(F32).rearrange("r (o t) -> r o t", o=1).broadcast_to((2 * H, HU, S))).then_inc(m_in[p][u], 16)

            sp.wait_ge(const_copied, 16)
            const_rows_in(0)
            rows_to_dram(0)
            sp.wait_ge(rows_out[0], 16)
            for half in range(2):
                stacks_in(0, 0, half)
            const_rows_in(1)
            for half in range(2):
                stacks_in(1, 1, half)
            for g in range(1, NG):
                rows_to_dram(g)
            m_rows_in(0, 0)
            sp.dma_start(down_w[:, 0:E, :], exp_Wdown.rearrange("e h i -> h e i")).then_inc(fw_in, 16)
            sp.dma_start(down_w[:, E, :], share_Wdown).then_inc(fw_in, 16)
            for n in range(2):
                sp.dma_start(down_b[3 * E + n:3 * E + n + 1, :], share_bdown.rearrange("(o d) -> o d", o=1)).then_inc(fw_in, 16)
            for n in range(3):
                sp.dma_start(down_b[E * n:E * n + E, :], exp_bdown).then_inc(fw_in, 16)
            sp.dma_start(part_signs[:], signs_c).then_inc(fw_in, 16)
            sp.dma_start(unit_rows[:], unit_c).then_inc(fw_in, 16)
            sp.dma_start(before[:], before_c).then_inc(fw_in, 16)
            sp.dma_start(rout_w[:], router_W.rearrange("c h e -> h c e")).then_inc(fw_in, 16)
            for dst, src in ((rout_b, router_b), (rout_gb, gate_bias), (norm_all, norm_w)):
                sp.dma_start(dst[:], src.rearrange("(o c) e -> o c e", o=1).broadcast_to((P, C, src.shape[1]))).then_inc(fw_in, 16)
            for g in range(1, NG):
                sp.wait_ge(rows_out[g], 16)
            with sp.Fori(1, B // 2) as pair:
                for p in range(2):
                    for half in range(2):
                        if half == 1:
                            m_rows_in(2 * pair + p - 1, 1 - p)
                        sp.wait_ge(st_done, 8 * (2 * pair + p - 2) + 4 * half + 4)
                        stacks_in(2 * pair + p, p, half)
            m_rows_in(B - 1, 1)
            out_tiles = out.rearrange("b (u p) d -> p (b u) d", p=P)
            for g in range(NG):
                sp.wait_ge(o_ready, g + 1)
                sp.dma_start(out_tiles[:, g * GT:g * GT + GT, :], xb_sb[:, g * GT:g * GT + GT, :]).then_inc(out_done, 16)
            sp.wait_ge(out_done, 16 * NG)

        @block.gpsimd
        def _(pool):
            start_from_1(pool, "pool")
            pool.memset(scale_one[:], QSCALE).then_inc(ones_ready, 1)
            pool.memset(step[:], 1.0).then_inc(ones_ready, 1)
            pool.memset(minus_half[:], -0.5).then_inc(ones_ready, 1)
            for p in range(2):
                for st in (q_st[p], k_st[p]):
                    pool.memset(st[:].bitcast(F32), 0.0).then_inc(st_zero, 1)
                pool.memset(v_st[p][:], 0.0).then_inc(v_const, 1)
                pool.wait_ge(v_const, 2 * p + 1)
                pool.memset(v_st[p][:, :, :, HD:HD + 1], 1.0).then_inc(v_const, 1)
            pool.wait_ge(ones_ready, 3)
            pool.wait_ge(v_const, 4)

            def stage_v(b, p):
                wait_from_1(pool, av_done, 4 * (b - 1))
                pool.tensor_copy(v_st[p][:, :, :, 0:HD], v_sb[:, bass.ds(b * TB, TB), :].rearrange("p t (h d) -> p t h d", h=H)).then_inc(v_ready, 1)

            def causal_select(n, r, half):
                pool.wait_ge(exp_done, 2 * n + half + 1)
                wait(pool, step_done, 2 * n + half)
                pool.tensor_tensor(step[:, 1:2], step[:, 0:1], step[:, 0:1], ALU.mult).then_inc(step_done, 1)
                v = probs[r][:, half * HU * S:half * HU * S + HU * (P if half else S)].rearrange("p (h q) -> p h q", h=HU)[:, :, 0:P]
                pool.affine_select(out=v, in_=v, compare_op=ALU.is_ge, fill=0.0, base=0,
                                   pattern=[[0, HU], [1, P]], channel_multiplier=-1).then_inc(sel_done, 1)

            def rstd(b):
                pool.wait_ge(var1_done, b + 1)
                pool.tensor_tensor(rstd1[:], var1[:], minus_half[:, 0:TB], ALU.pow).then_inc(rstd1_done, 1)

            def stage_x(group, q):
                wait_from_1(pool, x1_done, TB * group + TB)
                pool.tensor_copy(x_in[q][:], x1[:, bass.ds(group * GT, GT), :]).then_inc(xin_ready, 1)

            def batch(b, p, first, last):
                if last:
                    pool.wait_ge(st_done, 8 * (B - 1))
                    for q in range(2):
                        pool.memset(w_t[q][:].bitcast(F32), float(NS)).then_inc(wt_ready, 1)
                    stage_x(0, 0)
                for u in range(U):
                    for half in range(2):
                        causal_select(4 * b + u, u % 2, half)
                    if u == 1 and not last:
                        stage_v(b + 1, 1 - p)
                if not first:
                    rstd(b - 1)

            pool.wait_ge(v_copied, 1)
            stage_v(0, 0)
            pool.wait_ge(o_loaded, 32)
            pool.wait_ge(rows_out[2], 16)
            for g in range(NG):
                pool.wait_ge(x_loaded[g], 16)
                pool.tensor_tensor(xb_sb[:, GT * g:GT * g + GT, :], x_sb[:, GT * g:GT * g + GT, :],
                                   bo_all[:].rearrange("p (o d) -> p o d", o=1).broadcast_to((P, GT, D)), ALU.add).then_inc(xb_ready, 1)
            pool.wait_ge(v_copied, NG)
            batch(0, 0, True, False)
            with pool.Fori(0, B // 2 - 1) as pair:
                batch(2 * pair + 1, 1, False, False)
                batch(2 * pair + 2, 0, False, False)
            batch(B - 1, 1, False, True)
            stage_x(1, 1)
            rstd(B - 1)

            def power(dst, src, produced, count, done):
                wait_from_1(pool, produced, count)
                pool.tensor_tensor(dst[:], src[:], minus_half[:], ALU.pow).then_inc(done, 1)


            def rms(s):
                power(rms_inv, ms, ms_done, s + 1, rms_done)

            def rstd_end(g):
                power(rstd2, var2, var2_done, g + 1, rstd2_done)

            for s, (g, rnd) in enumerate(steps):
                wait_from_1(pool, hid_done, N * s + NS)
                pool.tensor_tensor(hid_sum[:], hid_s[0][:], hid_s[1][:], ALU.add).then_inc(hsum_done, 1)
                for e in range(E):
                    wait_from_1(pool, silu_done, N * s + NS + e + 1)
                    wait_from_1(pool, wb_copied, E * s + e + 1)
                    if e >= 2:
                        wait_from_1(pool, hid_done, N * s + NS + e - 1)
                    pool.tensor_tensor(silu_w[e % 2][:], silu[e % 2][:], wb_sb[e % 2][:], ALU.mult).then_inc(silu_w_done, 1)
                    if e == 0 and s:
                        rms(s - 1)
                    if e == 4 and s and steps[s - 1][1] == C - 1:
                        rstd_end(steps[s - 1][0])
                    if e == 5 and g + 2 < NG and (rnd, g % 2) in ((0, 1), (1, 0)):
                        stage_x(g + 1 if rnd == 0 else g + 3, rnd)
            rms(len(steps) - 1)
            rstd_end(NG - 1)

        @block.scalar
        def _(act):
            start_from_1(act, "act")
            act.dma_start(ident[:], ident_c).then_inc(ident_loaded, 16)
            act.dma_start(bq_row[:], bq.rearrange("(o d) -> o d", o=1)).then_inc(bq_loaded, 16)
            act.dma_start(w_in[:, 0, :], Wq).then_inc(w_loaded, 16)
            act.dma_start(causal[:], causal_c).then_inc(causal_loaded, 16)

            def x_high(g):
                act.wait_ge(xT_done, g + 1)
                wait(act, qkv_done, 3 * (g - 1))
                act.copy(xT_hi[:, g % 2, :], banks[:, g % 2, :]).then_inc(xhi_done, 1)

            x_high(0)
            act.wait_ge(bq_made, 1)
            act.copy(bq_col[:], banks[:, 7, 0:1]).then_inc(bq_ready, 1)
            x_high(1)
            act.wait_ge(bq_ready, 1)
            for g in range(NG):
                q_bank, k_bank, v_bank = (banks[:, n, :] for n in qkv_banks(g))
                act.wait_ge(qkv_done, 3 * g + 1)
                act.activation(qk_parts[g][:, 0, :], q_bank, ACT.Identity, bias=bq_col[:]).then_inc(qkh_done, 1)
                act.wait_ge(qkv_done, 3 * g + 2)
                act.copy(qk_parts[g][:, 3, :], k_bank).then_inc(qkh_done, 1)
                act.wait_ge(qkv_done, 3 * g + 3)
                act.copy(v_sb[:, GT * g:GT * g + GT, :].rearrange("p t d -> p (t d)"), v_bank).then_inc(v_copied, 1)
                if g + 2 < NG:
                    x_high(g + 2)

            def exps(n, r):
                for half, bank, lo, w in ((0, exp_bank0, 0, HU * S), (1, exp_bank1, HU * S, HU * P)):
                    act.wait_ge(st_done, 2 * n + half + 1)
                    if not half:
                        wait_from_1(act, av_done, n - 1)
                    act.activation(probs[r][:, lo:lo + w], bank, ACT.Exp).then_inc(exp_done, 1)

            def copy_av(b, p, u):
                n = 4 * b + u
                wait_from_1(act, av_done, n + 1)
                if u == 0:
                    wait_from_1(act, oT_done, 2 * (b - 1))
                act.copy(o_t[p][:, u, :], av_bank[u % 2]).then_inc(ot_copied, 1)

            def copy_m(b, p, before):
                act.wait_ge(mT_done, b + 1)
                for u in range(U):
                    wait(act, m_in[1 - p][u], 16 * before)
                act.copy(m_rows[:], mT_bank).then_inc(mT_copied, 1)

            def high_part(s, q):
                act.wait_ge(fT_done, s + 1)
                act.copy(f_hi[q][:], fT_bank).then_inc(fhi_done, 1)

            def batch(b, p, nth, first, last):
                if not first:
                    copy_av(b - 1, 1 - p, 3)
                exps(4 * b, 0)
                exps(4 * b + 1, 1)
                copy_av(b, p, 0)
                exps(4 * b + 2, 0)
                if not first:
                    copy_onT(b - 1)
                if last:
                    act.wait_ge(xin_ready, 1)
                    high_part(0, 0)
                copy_av(b, p, 1)
                exps(4 * b + 3, 1)
                if not last:
                    copy_m(b + 1, 1 - p, nth)
                copy_av(b, p, 2)

            def copy_onT(b):
                wait_from_1(act, onT_done, b + 1)
                wait_from_1(act, proj_done, b)
                act.copy(o_norm_t[:], misc[:, 0:S]).then_inc(onT_copied, 1)

            for half in range(2):
                act.wait_ge(upT_done, half + 1)
                act.copy(up_t[:, 4 * half:4 * half + 4, :].rearrange("p n i -> p (n i)"), banks[:, 5 + half, :]).then_inc(upT_copied, 1)
            act.wait_ge(bcol_done, 1)
            act.copy(b_cols[:], banks[:, 4, 0:2 * E + NS + 1]).then_inc(bcol_copied, 1)
            act.wait_ge(fw_first, 16 * FW_FIRST)
            act.copy(up_hi[:], up_w[:]).then_inc(fw_hi, 1)
            for half in range(2):
                act.wait_ge(wg_made, half + 1)
                act.copy(gate_hi[:, 4 * half:4 * half + 4, :].rearrange("p n i -> p (n i)"), banks[:, 5 + half, :]).then_inc(fw_hi, 1)


            copy_m(0, 0, 0)
            batch(0, 0, 1, True, False)
            with act.Fori(0, B // 2 - 1) as pair:
                batch(2 * pair + 1, 1, pair + 1, False, False)
                batch(2 * pair + 2, 0, pair + 2, False, False)
            batch(B - 1, 1, B // 2, False, True)
            def router_tanh(s):
                act.wait_ge(router_done, ROUTER_STEPS * s + ROUTER_STEPS - 4)
                act.activation(g_tanh[:], g_diff[:], ACT.Tanh).then_inc(tanh_done, 1)

            def weights_t(s, q):
                act.wait_ge(wT_done, s + 1)
                act.copy(w_t[q][0:3 * E, :], wT_bank).then_inc(wT_copied, 1)

            def copy_weights(s, e):
                act.wait_ge(wb_done, E * s + e + 1)
                wait_from_1(act, silu_w_done, E * s + e - 1)
                act.copy(wb_sb[e % 2][:], wb_bank).then_inc(wb_copied, 1)

            def silu_of(s, u):
                act.wait_ge(gate_done, N * s + u + 1)
                if u < NS:
                    wait_from_1(act, silu_w_done, E * s + u - 1)
                elif u < NS + 2:
                    wait_from_1(act, hid_done, N * s + u - 1)
                act.activation(silu[u % 2][:], gate_bank, ACT.Silu, bias=gate_b[:, weights_of(u):weights_of(u) + 1]).then_inc(silu_done, 1)

            copy_av(B - 1, 1, 3)
            silu_of(0, 0)
            router_tanh(0)
            copy_onT(B - 1)
            act.wait_ge(wt_ready, 2)
            for s, (g, rnd) in enumerate(steps):
                q = g % 2
                for u in range(1 if s == 0 else 0, N):
                    if u > NS:
                        copy_weights(s, u - NS)
                    if u == NS:
                        weights_t(s, q)
                    silu_of(s, u)
                    if u == 0:
                        router_tanh(s)
                    if u == NS:
                        copy_weights(s, 0)
                    if u == 5 and s + 1 < len(steps):
                        high_part(s + 1, 1 - q)

        @block.vector
        def _(dve):
            start_from_1(dve, "dve")
            dve.memset(causal_bf[:], 0.0).then_inc(warm_zero, 1)
            dve.wait_ge(bq_loaded, 16)
            dve.tensor_copy(bq_perm[:].rearrange("o (d h) -> o d h", h=H), bq_row[:].rearrange("o (h d) -> o d h", h=H)).then_inc(bq_cols, 1)
            dve.wait_ge(w_loaded, 48)
            dve.tensor_scalar(wqs[:], w_in[:, 0, :], QSCALE, None, ALU.mult).then_inc(wq_scaled, 1)
            dve.wait_ge(wq_scaled, 1)
            def cols(w, n):
                return w if n == 2 else w.rearrange("p (h d) -> p d h", h=H)

            def as_cols(w, n):
                return w if n == 2 else w.rearrange("p (d h) -> p d h", h=H)
            for n in range(3):
                src = wqs[:] if n == 0 else w_in[:, n, :]
                dve.tensor_copy(as_cols(w_hi[:, n, :], n), cols(src, n)).then_inc(w_split, 1)
                dve.wait_ge(w_split, 2 * n + 1)
                dve.tensor_tensor(as_cols(w_lo[:, n, :], n), cols(src, n), as_cols(w_hi[:, n, :].bitcast(F32), n), ALU.subtract).then_inc(w_split, 1)

            def x_low(g):
                dve.wait_ge(xhi_done, g + 1)
                dve.tensor_tensor(xT_lo[:, g % 2, :], banks[:, g % 2, :], xT_hi[:, g % 2, :].bitcast(F32), ALU.subtract).then_inc(xlo_done, 1)

            x_low(0)
            x_low(1)
            for g in range(NG):
                q_bank, k_bank, _ = (banks[:, n, :] for n in qkv_banks(g))
                if g == 0:
                    dve.wait_ge(bq_ready, 1)
                dve.wait_ge(qkh_done, 2 * g + 1)
                dve.scalar_tensor_tensor(out=qk_parts[g][:, 1, :], in0=q_bank, scalar=bq_col[:], in1=qk_parts[g][:, 0, :].bitcast(F32),
                                         op0=ALU.add, op1=ALU.subtract).then_inc(qkl_done, 1)
                dve.wait_ge(qkh_done, 2 * g + 2)
                dve.tensor_tensor(qk_parts[g][:, 2, :], k_bank, qk_parts[g][:, 3, :].bitcast(F32), ALU.subtract).then_inc(qkl_done, 1)
                if g + 2 < NG:
                    x_low(g + 2)
            dve.wait_ge(ident_loaded, 16)
            dve.tensor_copy(ident_bf[:], ident[:]).then_inc(cast_done, 1)
            dve.wait_ge(causal_loaded, 16)
            dve.tensor_copy(causal_bf[:], causal[:].rearrange("p (o d) -> p o d", o=1).broadcast_to((P, 4, P))).then_inc(cast_done, 1)

            def maxima(b, k):
                u, part = divmod(k, 3)
                dve.wait_ge(s_done, NBANK * b + k + 1)
                if k == 0:
                    wait(dve, m_lo, b)
                if part == 0:
                    dst, heads = m_neg[:, 0, HU * u:HU * u + HU], HU
                else:
                    h0 = HU * u + 2 * (part - 1)
                    dst, heads = m_neg[:, 1, h0:h0 + 2], 2
                dve.tensor_reduce(dst, max_bank[k % 2].rearrange("p (h k) -> p h k", h=heads), AX.X, ALU.max, negate=True).then_inc(max_done, 1)

            def split_m(b):
                dve.wait_ge(max_done, NBANK * (b + 1))
                wait(dve, mT_done, b)
                dve.tensor_copy(m_split[:, :, 0:H], m_neg[:]).then_inc(m_hi, 1)
                dve.wait_ge(m_hi, b + 1)
                dve.tensor_tensor(m_split[:, :, H:2 * H], m_neg[:], m_split[:, :, 0:H].bitcast(F32), ALU.subtract).then_inc(m_lo, 1)

            def normalise(b, t):
                wait_from_1(dve, oT_done, 2 * b + t + 1)
                o = misc.rearrange("p (h c) -> p h c", h=H)
                wait_from_1(dve, norm_done, 2 * b + t)
                dve.reciprocal(den_inv[:], o[:, :, HD]).then_inc(den_done, 1)
                dve.wait_ge(den_done, 2 * b + t + 1)
                if t == 0:
                    wait_from_1(dve, onT_done, b)
                dve.tensor_tensor(o_norm[:, t, :].rearrange("p (h d) -> p h d", h=H), o[:, :, 0:HD],
                                  den_inv[:].rearrange("p (h o) -> p h o", o=1).broadcast_to((P, H, HD)), ALU.mult).then_inc(norm_done, 1)

            def residual(b):
                wait_from_1(dve, proj_done, b + 1)
                wait_from_1(dve, x1_done, b)
                dve.tensor_tensor(res1[:], misc[:, 0:S].rearrange("p (t d) -> p t d", t=TB), xb_sb[:, bass.ds(b * TB, TB), :], ALU.add).then_inc(res1_done, 1)

            def moments(b):
                wait_from_1(dve, res1_done, b + 1)
                for t in range(TB):
                    last = dve.bn_stats(stats1[:, t, :], res1[:, t, :])
                last.then_inc(bn1_done, 1)
                dve.wait_ge(cast_done, 2)
                dve.wait_ge(bn1_done, b + 1)
                for t in range(TB):
                    last = dve.bn_aggr(mv1[:, t, :], stats1[:, t, :])
                last.then_inc(mv1_done, 1)
                dve.wait_ge(mv1_done, b + 1)
                wait_from_1(dve, rstd1_done, b)
                dve.tensor_scalar(var1[:], mv1[:, :, 1], LN_EPS, None, ALU.add).then_inc(var1_done, 1)

            def layernorm(b):
                wait_from_1(dve, rstd1_done, b + 1)
                for t in range(TB):
                    last = dve.tensor_scalar(x1[:, bass.ds(b * TB + t, 1), :].rearrange("p o d -> p (o d)"), res1[:, t, :], mv1[:, t, 0:1], rstd1[:, t:t + 1], ALU.subtract, ALU.mult)
                last.then_inc(x1_done, 1)

            def low_part(s, q):
                dve.wait_ge(fhi_done, s + 1)
                dve.tensor_tensor(f_lo[q][:], fT_bank, f_hi[q][:].bitcast(F32), ALU.subtract).then_inc(flo_done, 1)

            def over_tiles(row):
                return row.rearrange("p (o e) -> p o e", o=1).broadcast_to((P, GT, E))

            def route(s, rnd, halves):
                done_before = 0

                def done(ins):
                    nonlocal done_before
                    done_before += 1
                    ins.then_inc(router_done, 1)

                def ready():
                    dve.wait_ge(router_done, ROUTER_STEPS * s + done_before)

                if 0 in halves:
                    dve.wait_ge(gates_done, s + 1)
                    parts = rout_bank.rearrange("p (t e) -> p t e", t=GT)
                    done(dve.tensor_tensor(g_part[:], parts[:, :, 0:E], over_tiles(rout_b[:, rnd, :]), ALU.add))
                    ready()
                    done(dve.tensor_tensor(g_val[:], g_part[:], parts[:, :, E:2 * E], ALU.add))
                    ready()
                    done(dve.tensor_tensor(g_bias[:], g_val[:], over_tiles(rout_gb[:, rnd, :]), ALU.add))
                    ready()
                    other = g_bias[:].rearrange("p t (o e) -> p t o e", o=1).broadcast_to((P, GT, E, E))
                    own = g_bias[:].rearrange("p t (e o) -> p t e o", o=1).broadcast_to((P, GT, E, E))
                    done(dve.tensor_tensor(beats[:], other, own, ALU.is_gt))
                    done(dve.tensor_tensor(ties[:], other, own, ALU.is_equal))
                    ready()
                    flat = ties[:].rearrange("p t e f -> p t (e f)")
                    done(dve.tensor_tensor(flat, flat, before[:].rearrange("p (o n) -> p o n", o=1).broadcast_to((P, GT, E * E)), ALU.mult))
                    assert done_before == ROUTER_FIRST
                if 1 in halves:
                    done_before = ROUTER_FIRST
                    ready()
                    done(dve.tensor_tensor(beats[:], beats[:], ties[:], ALU.add))
                    ready()
                    done(dve.tensor_reduce(rank[:], beats[:], AX.X, ALU.add))
                if 2 in halves:
                    done_before = ROUTER_FIRST + 2
                    ready()
                    done(dve.tensor_scalar(half_sel[:], rank[:], float(TOPK), 0.5, ALU.is_lt, ALU.mult))
                    ready()
                    done(dve.tensor_tensor(sel_g[:], half_sel[:], g_val[:], ALU.mult))
                    ready()
                    done(dve.tensor_reduce(half_sum[:], sel_g[:], AX.X, ALU.add))
                    ready()
                    done(dve.tensor_tensor(g_diff[:], g_val[:], half_sum[:].rearrange("p (t o) -> p t o", o=1).broadcast_to((P, GT, E)), ALU.subtract))
                    assert done_before == ROUTER_STEPS - 4

            def batch(b, behind, last):
                for k in range(NBANK):
                    if not last:
                        maxima(b + 1, k)
                    if k == 1 and behind > 1:
                        layernorm(b - 2)
                    if k in (3, 6) and behind:
                        normalise(b - 1, k // 4)
                if not last:
                    split_m(b + 1)
                if last:
                    low_part(0, 0)
                if behind:
                    residual(b - 1)
                    moments(b - 1)
                if last:
                    route(0, 0, range(3))

            dve.wait_ge(fw_first, 16 * FW_FIRST)
            dve.wait_ge(fw_hi, 1)
            dve.tensor_tensor(up_lo[:], up_w[:], up_hi[:].bitcast(F32), ALU.subtract).then_inc(fw_lo, 1)
            for half in range(2):
                dve.wait_ge(fw_hi, 2 + half)
                dve.tensor_tensor(gate_lo[:, 4 * half:4 * half + 4, :].rearrange("p n i -> p (n i)"), banks[:, 5 + half, :],
                                  gate_hi[:, 4 * half:4 * half + 4, :].rearrange("p n i -> p (n i)").bitcast(F32), ALU.subtract).then_inc(fw_lo, 1)
            dve.wait_ge(bg_made, 1)
            dve.tensor_tensor(gate_b[:, 0:E], banks[:, 4, 0:E], b_cols[:, E:2 * E], ALU.add).then_inc(gb_ready, 1)
            dve.tensor_scalar(gate_b[:, E:N], banks[:, 4, E:N], b_cols[:, 2 * E + NS:2 * E + NS + 1], None, ALU.add).then_inc(gb_ready, 1)

            for k in range(NBANK):
                maxima(0, k)
            split_m(0)

            batch(0, 0, False)
            dve.wait_ge(xb_ready, NG)
            dve.wait_ge(rows_out[3], 16)
            dve.wait_ge(fw_in, 16 * FW_REST)
            dve.tensor_copy(unit_rows_r[:], unit_rows[:].rearrange("p (e i) -> p e i", e=E)).then_inc(rw_split, 1)
            dve.tensor_copy(rout_parts[:, :, 0:E], rout_w[:]).then_inc(rw_split, 1)
            dve.tensor_copy(down_b_hi[:], down_b[:]).then_inc(rw_split, 1)
            dve.tensor_scalar(down_b_lo[:], down_b[:], part_signs[:, 1:2], None, ALU.mult).then_inc(rw_split, 1)
            dve.wait_ge(rw_split, 4)
            dve.tensor_tensor(rout_parts[:, :, E:2 * E], rout_w[:], rout_parts[:, :, 0:E].bitcast(F32), ALU.subtract).then_inc(rw_split, 1)
            dve.scalar_tensor_tensor(out=down_b_parts[:], in0=down_b_hi[:].bitcast(F32), scalar=part_signs[:, 0:1], in1=down_b_lo[:],
                                     op0=ALU.mult, op1=ALU.add).then_inc(rw_split, 1)
            batch(1, 1, False)
            with dve.Fori(2, B - 1) as b:
                batch(b, 2, False)
            batch(B - 1, 2, True)
            def weigh(s):
                dve.wait_ge(tanh_done, s + 1)
                for dst in (w_tok[:], w_tok_s[:, :, 0:E], w_tok_s[:, :, 2 * E:3 * E]):
                    dve.scalar_tensor_tensor(out=dst, in0=g_tanh[:], scalar=1.0, in1=half_sel[:], op0=ALU.add, op1=ALU.mult).then_inc(router_done, 1)
                dve.wait_ge(router_done, ROUTER_STEPS * s + ROUTER_STEPS - 1)
                dve.tensor_tensor(w_tok_s[:, :, E:2 * E], w_tok[:], w_tok_s[:, :, 0:E].bitcast(F32), ALU.subtract).then_inc(router_done, 1)

            def unit(s, u):
                e = weights_of(u)
                up_b = b_cols[:, e:e + 1] if e < E else b_cols[:, E + e:E + e + 1]
                if u < NS:
                    wait_from_1(dve, silu_done, N * s + u + 1)
                    dst, factor = hid_s[u], silu[u]
                else:
                    wait_from_1(dve, silu_w_done, E * s + e + 1)
                    if e >= 2:
                        wait_from_1(dve, down_done, (E + 1) * s + e)
                    dst, factor = hid_w[e % 2], silu_w[e % 2]
                dve.wait_ge(up_done, N * s + u + 1)
                dve.scalar_tensor_tensor(out=dst[:], in0=up_bank[u % 2], scalar=up_b, in1=factor[:], op0=ALU.add, op1=ALU.mult).then_inc(hid_done, 1)

            layernorm(B - 2)
            normalise(B - 1, 0)
            normalise(B - 1, 1)
            weigh(0)
            unit(0, 0)
            residual(B - 1)
            moments(B - 1)
            unit(0, 1)
            layernorm(B - 1)

            def add_residual(s, g, q, rnd):
                wait_from_1(dve, down_done, (E + 1) * (s + 1))
                src = x1[:, g * GT:g * GT + GT, :] if rnd == 0 else y_out[q][:]
                dve.tensor_tensor(y_sum[q][:], down_bank[q].rearrange("p (t d) -> p t d", t=GT), src, ALU.add).then_inc(ysum_done, 1)

            def mean_square(s, q):
                wait_from_1(dve, ysum_done, s + 1)
                for t in range(GT):
                    last = dve.tensor_tensor_reduce(out=squares[:, t, :], in0=y_sum[q][:, t, :], in1=y_sum[q][:, t, :], scale=1.0 / D, scalar=FF_EPS,
                                                    op0=ALU.mult, op1=ALU.add, accum_out=ms[:, t:t + 1])
                last.then_inc(ms_done, 1)

            def rms_norm(s, q):
                dve.wait_ge(rms_done, s + 1)
                for t in range(GT):
                    last = dve.scalar_tensor_tensor(out=y_out[q][:, t, :], in0=y_sum[q][:, t, :], scalar=rms_inv[:, t:t + 1], in1=norm_all[:, 0, :], op0=ALU.mult, op1=ALU.mult)
                last.then_inc(y_done, 1)

            def end_scale(q):
                dve.tensor_tensor(y_end[q][:], y_sum[q][:], norm_all[:, C - 1, :].rearrange("p (o d) -> p o d", o=1).broadcast_to((P, GT, D)), ALU.mult).then_inc(y_done, 1)

            def end_residual(s, g, q):
                dve.wait_ge(y_done, s + 1)
                dve.wait_ge(rms_done, s + 1)
                for t in range(GT):
                    last = dve.scalar_tensor_tensor(out=x_end[q][:, t, :], in0=y_end[q][:, t, :], scalar=rms_inv[:, t:t + 1], in1=x1[:, g * GT + t, :], op0=ALU.mult, op1=ALU.add)
                last.then_inc(xend_done, 1)

            def end_moments(g, q):
                wait_from_1(dve, xend_done, g + 1)
                for t in range(GT):
                    last = dve.bn_stats(stats2[:, t, :], x_end[q][:, t, :])
                last.then_inc(bn2_done, 1)
                dve.wait_ge(cast_done, 2)
                wait_from_1(dve, bn2_done, g + 1)
                for t in range(GT):
                    last = dve.bn_aggr(mv2[:, t, :], stats2[:, t, :])
                last.then_inc(mv2_done, 1)
                dve.wait_ge(mv2_done, g + 1)
                dve.tensor_scalar(var2[:], mv2[:, :, 1], LN_EPS, None, ALU.add).then_inc(var2_done, 1)
                dve.tensor_tensor(y_end[q][:], x_end[q][:], mv2[:, :, 0:1].broadcast_to((P, GT, D)), ALU.subtract).then_inc(centred, 1)

            def end_norm(g, q):
                dve.wait_ge(centred, g + 1)
                dve.wait_ge(rstd2_done, g + 1)
                dve.tensor_tensor(xb_sb[:, g * GT:g * GT + GT, :], y_end[q][:], rstd2[:].rearrange("p (t o) -> p t o", o=1).broadcast_to((P, GT, D)), ALU.mult).then_inc(o_ready, 1)

            def behind(s, u):
                g, rnd = steps[s]
                q = g % 2
                if u == 0:
                    add_residual(s, g, q, rnd)
                if u == 1:
                    mean_square(s, q)
                if rnd < C - 1:
                    if u == 3:
                        rms_norm(s, q)
                else:
                    if u == 1:
                        end_scale(q)
                    if u == 3:
                        end_residual(s, g, q)
                    if u == 4:
                        end_moments(g, q)
                    if u == 6:
                        end_norm(g, q)

            for s, (g, rnd) in enumerate(steps):
                for u in range(2 if s == 0 else 0, N):
                    if u == 0:
                        weigh(s)
                    unit(s, u)
                    if u == 4 and s + 1 < len(steps):
                        low_part(s + 1, 1 - g % 2)
                    if s:
                        behind(s - 1, u)
                    if u in (5, 6, 7) and s + 1 < len(steps):
                        route(s + 1, steps[s + 1][1], (u - 5,))
            for u in range(N):
                behind(len(steps) - 1, u)

        @block.tensor
        def _(pe):
            start_from_1(pe, "pe")
            PASSES = ((w_hi, xT_hi), (w_hi, xT_lo), (w_lo, xT_hi))

            def transpose_x(g):
                pe.wait_ge(x_loaded[g], 16)
                wait(pe, xlo_done, g - 1)
                for t in range(GT):
                    last = pe.transpose(banks[:, g % 2, P * t:P * t + P], x_sb[:, GT * g + t, :], ident[:])
                last.then_inc(xT_done, 1)

            def keep_warm(n, stationary, bank):
                for _ in range(n):
                    pe.matmul(banks[:, bank, :], stationary, causal_bf[:].rearrange("p n k -> p (n k)"))

            pe.wait_ge(warm_zero, 1)
            keep_warm(WARM_FIRST, causal_bf[:, 0, :], 2)
            pe.wait_ge(ident_loaded, 16)
            transpose_x(0)
            pe.wait_ge(ones_ready, 1)
            pe.wait_ge(bq_cols, 1)
            pe.matmul(banks[:, 7, 0:1], bq_perm[:], scale_one[:]).then_inc(bq_made, 1)
            transpose_x(1)
            keep_warm(WARM_SPLITS, causal_bf[:, 0, :], 2)
            pe.wait_ge(w_split, 6)
            pe.wait_ge(bq_ready, 1)
            for g in range(NG):
                q_bank, k_bank, v_bank = qkv_banks(g)
                pe.wait_ge(xhi_done, g + 1)
                pe.wait_ge(xlo_done, g + 1)
                for n, bank in enumerate((q_bank, k_bank)):
                    wait(pe, qkl_done, 2 * (g - 2) + n + 1)
                    for k, (w, xt) in enumerate(PASSES):
                        last = pe.matmul(banks[:, bank, :], w[:, n, :], xt[:, g % 2, :], start=(k == 0), stop=(k == 2))
                    last.then_inc(qkv_done, 1)
                wait(pe, v_copied, g - 1)
                for t in range(GT):
                    for k, (w, xt) in enumerate(PASSES):
                        last = pe.matmul(banks[:, v_bank, P * t:P * t + P], xt[:, g % 2, P * t:P * t + P], w[:, 2, :], start=(k == 0), stop=(k == 2))
                last.then_inc(qkv_done, 1)
                if g + 2 < NG:
                    transpose_x(g + 2)

            def scores_for_max(b, p, nth, k):
                u, part = divmod(k, 3)
                if k in (0, NBANK // 2):
                    pe.wait_ge(st_in[p][u // 2], 16 * 4 * nth)
                wait(pe, max_done, NBANK * b + k - 1)
                bank = max_bank[k % 2]
                if part == 0:
                    heads, width, keys, q0 = HU, P, P, 0
                else:
                    heads, width, keys, q0 = 2, S, S, P
                pe.matmul(bank.rearrange("p (h k) -> p h k", h=heads)[:, :, width - P:width], ident_bf[:], causal_bf[:, 0:heads, :],
                          start=True, stop=False, skip_group_check=True)
                for j in range(heads):
                    h = HU * u + 2 * max(part - 1, 0) + j
                    last = pe.matmul(bank[:, width * j:width * (j + 1)], q_st[p][0:ROWS_MAX, h, q0:q0 + P], k_st[p][0:ROWS_MAX, h, 0:keys],
                                     start=False, stop=True, skip_group_check=True)
                last.then_inc(s_done, 1)

            def scores_for_exp(b, p, nth, u):
                n = 4 * b + u
                pe.wait_ge(m_in[p][u], 16 * nth)
                wait(pe, exp_done, 2 * n - 1)
                for j in range(HU):
                    h = HU * u + j
                    last = pe.matmul(exp_bank0[:, S * j:S * j + S], k_st[p][0:ROWS_EXP, h, 0:P], q_st[p][0:ROWS_EXP, h, :])
                last.then_inc(st_done, 1)
                wait(pe, exp_done, 2 * n)
                for j in range(HU):
                    h = HU * u + j
                    last = pe.matmul(exp_bank1[:, P * j:P * j + P], k_st[p][0:ROWS_EXP, h, P:S], q_st[p][0:ROWS_EXP, h, P:S])
                last.then_inc(st_done, 1)

            def product_with_v(b, p, u):
                n = 4 * b + u
                r = u % 2
                if u == 0:
                    pe.wait_ge(v_ready, b + 1)
                wait(pe, ot_copied, n - 1)
                if u == 3:
                    pe.wait_ge(mT_copied, min(b + 2, B) if isinstance(b, int) else b + 2)
                pe.wait_ge(sel_done, 2 * n + 1)
                for j in range(HU):
                    pe.matmul(av_bank[r][32 * j:32 * j + 32, :], v_st[p][:, 0, HU * u + j, :], probs[r][:, S * j:S * j + S],
                              start=True, stop=False, skip_group_check=True, tile_position=(0, 32 * j))
                pe.wait_ge(sel_done, 2 * n + 2)
                for j in range(HU):
                    last = pe.matmul(av_bank[r][32 * j:32 * j + 32, P:S], v_st[p][:, 1, HU * u + j, :], probs[r][:, HU * S + P * j:HU * S + P * j + P],
                                     start=False, stop=True, skip_group_check=True, tile_position=(0, 32 * j))
                last.then_inc(av_done, 1)

            def transpose_m(b):
                pe.wait_ge(m_lo, b + 1)
                wait(pe, mT_copied, b)
                wait(pe, ot_copied, 4 * b - 2)
                for t in range(TB):
                    last = pe.transpose(mT_bank[:, P * t:P * t + P], m_split[:, t, :].bitcast(F32), ident[:])
                last.then_inc(mT_done, 1)

            def transpose_o(b, p, t):
                if t == 0:
                    pe.wait_ge(ot_copied, 4 * (b + 1))
                    wait_from_1(pe, res1_done, b)
                else:
                    wait_from_1(pe, norm_done, 2 * b + 1)
                for u in range(U):
                    last = pe.transpose(misc[:, P * u:P * u + P], o_t[p][:, u, P * t:P * t + P], ident[:])
                last.then_inc(oT_done, 1)

            def transpose_norm(b):
                wait_from_1(pe, norm_done, 2 * b + 2)
                for t in range(TB):
                    last = pe.transpose(misc[:, P * t:P * t + P], o_norm[:, t, :], ident[:])
                last.then_inc(onT_done, 1)

            def project(b):
                pe.wait_ge(onT_copied, b + 1)
                for t in range(TB):
                    last = pe.matmul(misc[:, P * t:P * t + P], o_norm_t[:, P * t:P * t + P], wo[:])
                last.then_inc(proj_done, 1)

            def three_passes(bank, w_h, w_l, q, done):
                for k, (w, f) in enumerate(((w_h, f_hi), (w_h, f_lo), (w_l, f_hi))):
                    last = pe.matmul(bank, w, f[q][:], start=(k == 0), stop=(k == 2))
                last.then_inc(done, 1)

            def transposes(s, q, src, produced, count):
                pe.wait_ge(produced, count)
                wait_from_1(pe, flo_done, s)
                for t in range(GT):
                    last = pe.transpose(fT_bank[:, P * t:P * t + P], src[:, t, :], ident[:])
                last.then_inc(fT_done, 1)

            def gate(s, q, u):
                wait_from_1(pe, silu_done, N * s + u)
                three_passes(gate_bank, gate_hi[:, weights_of(u), :], gate_lo[:, weights_of(u), :], q, gate_done)

            def gates(s, q, rnd):
                pe.wait_ge(fhi_done, s + 1)
                wait_from_1(pe, flo_done, s + 1)
                for t in range(GT):
                    at = 2 * E * t
                    token_hi, token_lo = (f[q][:, P * t:P * t + P] for f in (f_hi, f_lo))
                    pe.matmul(rout_bank[:, at:at + 2 * E], token_hi, rout_parts[:, rnd, :], start=True, stop=False, skip_group_check=True)
                    last = pe.matmul(rout_bank[:, at:at + E], token_lo, rout_parts[:, rnd, 0:E], start=False, stop=True, skip_group_check=True)
                last.then_inc(gates_done, 1)

            def weights_t(s):
                pe.wait_ge(router_done, ROUTER_STEPS * (s + 1))
                wait_from_1(pe, wT_copied, s)
                for t in range(GT):
                    last = pe.transpose(wT_bank[:, P * t:P * t + P], w_tok_s[:, t, :].bitcast(F32), ident[:])
                last.then_inc(wT_done, 1)

            def down(s, q, tile, w, first, last_one):
                for t in range(GT):
                    last = pe.matmul(down_bank[q][:, P * t:P * t + P], tile[:, P * t:P * t + P], w, start=(first and t == 0), stop=last_one, skip_group_check=True)
                return last


            def batch(b, p, nth, first, last):
                def maxima(*ks):
                    if not last:
                        for k in ks:
                            scores_for_max(b + 1, 1 - p, nth + p, k)

                maxima(0)
                if not first:
                    product_with_v(b - 1, 1 - p, 3)
                maxima(1, 2)
                if not first:
                    transpose_o(b - 1, 1 - p, 0)
                scores_for_exp(b, p, nth, 0)
                maxima(3, 4)
                scores_for_exp(b, p, nth, 1)
                maxima(5)
                if last:
                    transposes(0, 0, x_in[0], xin_ready, 1)
                if not first:
                    transpose_o(b - 1, 1 - p, 1)
                product_with_v(b, p, 0)
                maxima(6, 7)
                scores_for_exp(b, p, nth, 2)
                if not first:
                    transpose_norm(b - 1)
                maxima(8, 9)
                product_with_v(b, p, 1)
                maxima(10)
                if not first:
                    project(b - 1)
                maxima(11)
                scores_for_exp(b, p, nth, 3)
                if last:
                    pe.wait_ge(rw_split, 6)
                    gates(0, 0, 0)
                if not last:
                    transpose_m(b + 1)
                product_with_v(b, p, 2)

            pe.wait_ge(xlo_done, NG)
            pe.wait_ge(qkl_done, 2 * NG)
            pe.wait_ge(v_copied, NG)

            pe.wait_ge(fw_first, 16 * FW_FIRST)
            for half in range(2):
                for n in range(4):
                    last = pe.transpose(banks[:, 5 + half, P * n:P * n + P], up_w[:, 4 * half + n, :], ident[:])
                last.then_inc(upT_done, 1)
            pe.transpose(banks[:, 4, 0:2 * E + NS + 1], b_rows[:], ident[0:2 * E + NS + 1, 0:2 * E + NS + 1]).then_inc(bcol_done, 1)
            for half in range(2):
                pe.wait_ge(upT_copied, half + 1)
                for n in range(4):
                    e = 4 * half + n
                    last = pe.matmul(banks[:, 5 + half, P * n:P * n + P], up_t[:, e, :], gate_w[:, min(e, E), :])
                last.then_inc(wg_made, 1)
            pe.wait_ge(bcol_copied, 1)
            for e in range(N):
                col = e if e < E else E + e
                last = pe.matmul(banks[:, 4, e:e + 1], gate_w[:, min(e, E), :], b_cols[:, col:col + 1])
            last.then_inc(bg_made, 1)
            pe.wait_ge(cast_done, 2)
            pe.wait_ge(const_in[0], 16 * 3)
            for k in range(NBANK):
                scores_for_max(0, 0, 1, k)
            transpose_m(0)

            pe.wait_ge(const_in[1], 16 * 3)
            pe.wait_ge(fw_lo, 3)
            pe.wait_ge(gb_ready, 2)
            pe.wait_ge(o_loaded, 32)
            batch(0, 0, 1, True, False)
            with pe.Fori(0, B // 2 - 1) as pair:
                batch(2 * pair + 1, 1, pair + 1, False, False)
                batch(2 * pair + 2, 0, pair + 2, False, False)
            batch(B - 1, 1, B // 2, False, True)
            def up(s, q, u):
                wait_from_1(pe, hid_done, N * s + u - 1)
                three_passes(up_bank[u % 2], up_hi[:, weights_of(u), :], up_lo[:, weights_of(u), :], q, up_done)

            def expert_weights(s, q, e):
                wait_from_1(pe, wb_copied, E * s + e)
                pe.matmul(wb_bank, unit_rows_r[:, e, :], w_t[q][0:2 * E, :]).then_inc(wb_done, 1)

            def down_expert(s, q, e):
                wait_from_1(pe, hid_done, N * s + NS + e + 1)
                down(s, q, hid_w[e % 2], down_w[:, e, :], False, e == E - 1).then_inc(down_done, 1)

            product_with_v(B - 1, 1, 3)
            pe.wait_ge(exp_done, 8 * B)
            gate(0, 0, 0)
            transpose_o(B - 1, 1, 0)
            up(0, 0, 0)
            transpose_o(B - 1, 1, 1)
            gate(0, 0, 1)
            transpose_norm(B - 1)
            keep_warm(WARM_END, ident_bf[:], 0)
            project(B - 1)

            pe.wait_ge(fw_in, 16 * FW_REST)
            pe.wait_ge(ot_copied, 4 * B)
            for s, (g, rnd) in enumerate(steps):
                q = g % 2
                for u in range(1 if s == 0 else 0, N):
                    if NS + 1 < u + 1 < N:
                        expert_weights(s, q, u + 1 - NS)
                    if u == 1:
                        weights_t(s)
                    if u + 1 < N:
                        gate(s, q, u + 1)
                    if u == N - 1 and s + 1 < len(steps):
                        gate(s + 1, 1 - q, 0)
                    if u == NS:
                        expert_weights(s, q, 1)
                    up(s, q, u)
                    if u == 0:
                        if s:
                            down_expert(s - 1, 1 - q, E - 1)
                    elif u == 1:
                        wait_from_1(pe, wT_copied, s + 1)
                        expert_weights(s, q, 0)
                        if s == 0:
                            wait_from_1(pe, res1_done, B)
                        wait_from_1(pe, ysum_done, s - 1)
                        down(s, q, w_t[q], down_b_parts[:], True, False)
                    elif u == 2:
                        pe.wait_ge(hsum_done, s + 1)
                        down(s, q, hid_sum, down_w[:, E, :], False, False).then_inc(down_done, 1)
                    else:
                        down_expert(s, q, u - 3)
                    if u == 4 and s + 1 < len(steps):
                        next_g, next_rnd = steps[s + 1]
                        if next_rnd == 0:
                            transposes(s + 1, 1 - q, x_in[1 - q], xin_ready, next_g + 1)
                        else:
                            transposes(s + 1, 1 - q, y_out[1 - q], y_done, s)
                    if u == 5 and s + 1 < len(steps):
                        gates(s + 1, 1 - q, steps[s + 1][1])
            down_expert(len(steps) - 1, 1, E - 1)


_INS = ['L0_attn_x', 'L0_attn_Wq', 'L0_attn_bq', 'L0_attn_Wk', 'L0_attn_Wv', 'L0_attn_Wo', 'L0_attn_bo',
        'L0_ffn_router_W', 'L0_ffn_router_b', 'L0_ffn_gate_bias', 'L0_ffn_exp_Wup', 'L0_ffn_exp_bup', 'L0_ffn_exp_Wg', 'L0_ffn_exp_bg',
        'L0_ffn_exp_Wdown', 'L0_ffn_exp_bdown', 'L0_ffn_share_Wup', 'L0_ffn_share_bup', 'L0_ffn_share_Wg', 'L0_ffn_share_bg',
        'L0_ffn_share_Wdown', 'L0_ffn_share_bdown', 'L0_ffn_norm_w']


def constants():
    import numpy as np
    ident = np.eye(P, dtype=np.float32)
    causal = np.where(np.arange(P)[None, :] > np.arange(P)[:, None], np.float32(-1e30), np.float32(0)).astype(np.float32)
    slopes = (2.0 ** (-8.0 * np.arange(1, H + 1, dtype=np.float32) / H)).astype(np.float32)
    alibi = -(slopes[:, None] * np.arange(S, dtype=np.float32)[None, :]).astype(np.float32)
    hi = (alibi.view(np.uint32) & np.uint32(0xFFFFF000)).view(np.float32)
    of_head = np.zeros((2, H, H, S), np.float32)
    for h in range(H):
        of_head[:, h, h, :] = 1
    rows = np.concatenate([hi[None], (alibi - hi)[None], np.ones((2, H, S), np.float32), of_head.reshape(2 * H, H, S)])
    unit = np.zeros((2, E, E, P), np.float32)
    for e in range(E):
        unit[:, e, e, :] = 1
    before = np.zeros((P, E, E), np.float32)
    before[:] = np.arange(E)[None, :] < np.arange(E)[:, None]
    is_lo = np.zeros(BIAS_ROWS, np.float32)
    is_lo[2 * E:3 * E] = is_lo[3 * E + 1] = 1
    signs = np.stack([1 - 2 * is_lo, is_lo], 1)
    return {"ident_c": ident, "causal_c": causal, "alibi_c": rows, "unit_c": unit.reshape(2 * E, E * P),
            "before_c": before.reshape(P, E * E), "signs_c": signs}


def kernel(**inputs):
    import numpy as _np
    import concourse.bacc as _bacc
    from concourse import mybir as _mybir
    from concourse.bass_utils import run_bass_kernel_spmd as _run

    nc = _bacc.Bacc("TRN2", target_bir_lowering=False, num_devices=1)
    arrays, args = {}, []
    for name, a in [(n, inputs[n]) for n in _INS] + list(constants().items()):
        a = _np.ascontiguousarray(a)
        arrays[f"in_{name}_dram"] = a
        args.append(nc.dram_tensor(f"in_{name}_dram", a.shape, _mybir.dt.from_np(a.dtype), kind="ExternalInput").ap())
    args.append(nc.dram_tensor("out_0_dram", (B, S, D), F32, kind="ExternalOutput").ap())
    program(nc, *args)
    r = _run(nc, [arrays], core_ids=[0])
    return r.results[0]["out_0_dram"]
```
